# Optimizing a Trainium2 kernel written in Bass

```python
import numpy as np
import jax
import jax.numpy as jnp

def _softmax(x, axis=-1):
    return jax.nn.softmax(x, axis=axis)

def _gelu(x):
    return jax.nn.gelu(x, approximate=True)

def _silu(x):
    return jax.nn.silu(x)

def _sigmoid(x):
    return jax.nn.sigmoid(x)

def _layernorm(x, axis=-1, eps=1e-05):
    m = jnp.mean(x, axis=axis, keepdims=True)
    v = jnp.var(x, axis=axis, keepdims=True)
    return (x - m) / jnp.sqrt(v + eps)

def _scatter_add(tgt, idx, src, axis=0):
    return tgt.at[idx].add(src)

def _segment_sum(src, seg, n):
    return jax.ops.segment_sum(src, seg, n)
kernel_name = 'mk_macaron_d1_jaxref_r8_d13f30'

def setup_inputs(seed: int=0):
    np.random.seed(seed)
    _w = jnp.asarray

    def _L0_attn_setup():
        import jax, jax.numpy as jnp
        import numpy as np
        from jax import lax
        BLOCK_LEN = 128
        NEG_INF = -1000000000.0
        key = jax.random.key(seed)
        ks = jax.random.split(key, 8)
        N, L, Dm = (2, 1024, 512)
        W, H, dh = (128, 16, 64)
        s = lambda fan: 1.0 / np.sqrt(fan)
        return {'inputs': jax.random.normal(ks[0], (N, L, Dm), jnp.float32), 'conv_w': jax.random.normal(ks[1], (3, Dm, 3 * W), jnp.float32) * s(3 * Dm), 'conv_b': jnp.zeros((3 * W,), jnp.float32), 'wq': jax.random.normal(ks[2], (W, H, dh), jnp.float32) * s(W), 'bq': jnp.zeros((H, dh), jnp.float32), 'wk': jax.random.normal(ks[3], (W, H, dh), jnp.float32) * s(W), 'bk': jnp.zeros((H, dh), jnp.float32), 'wv': jax.random.normal(ks[4], (W, H, dh), jnp.float32) * s(W), 'bv': jnp.zeros((H, dh), jnp.float32), 'wo': jax.random.normal(ks[5], (H, dh, W), jnp.float32) * s(H * dh), 'bo': jnp.zeros((W,), jnp.float32), 'proj_w': jax.random.normal(ks[6], (W, Dm), jnp.float32) * s(W), 'proj_b': jnp.zeros((Dm,), jnp.float32)}
    _L0_attn_in = _L0_attn_setup()

    def _L0_ffn_setup():
        import jax, jax.numpy as jnp
        import numpy as np
        HID, INTER = (512, 1792)
        B, S = (2, 256)

        def _binary_diff_weight(w, base):
            d = w - base
            coeff = jnp.mean(jnp.abs(d))
            return base + coeff * jnp.sign(d)
        key = jax.random.key(seed)
        ks = jax.random.split(key, 7)
        return {'hidden_states': jax.random.normal(ks[0], (B, S, HID), dtype=jnp.float32), 'w1': jax.random.normal(ks[1], (INTER, HID), dtype=jnp.float32) * 0.02, 'mean_w1': jax.random.normal(ks[2], (INTER, HID), dtype=jnp.float32) * 0.02, 'w2': jax.random.normal(ks[3], (HID, INTER), dtype=jnp.float32) * 0.02, 'mean_w2': jax.random.normal(ks[4], (HID, INTER), dtype=jnp.float32) * 0.02, 'w3': jax.random.normal(ks[5], (INTER, HID), dtype=jnp.float32) * 0.02, 'mean_w3': jax.random.normal(ks[6], (INTER, HID), dtype=jnp.float32) * 0.02}
    _L0_ffn_in = _L0_ffn_setup()
    _d = {'L0_attn_inputs': _L0_attn_in['inputs'], 'L0_attn_conv_w': _L0_attn_in['conv_w'], 'L0_attn_conv_b': _L0_attn_in['conv_b'], 'L0_attn_wq': _L0_attn_in['wq'], 'L0_attn_bq': _L0_attn_in['bq'], 'L0_attn_wk': _L0_attn_in['wk'], 'L0_attn_bk': _L0_attn_in['bk'], 'L0_attn_wv': _L0_attn_in['wv'], 'L0_attn_bv': _L0_attn_in['bv'], 'L0_attn_wo': _L0_attn_in['wo'], 'L0_attn_bo': _L0_attn_in['bo'], 'L0_attn_proj_w': _L0_attn_in['proj_w'], 'L0_attn_proj_b': _L0_attn_in['proj_b'], 'L0_ffn_w1': _L0_ffn_in['w1'], 'L0_ffn_mean_w1': _L0_ffn_in['mean_w1'], 'L0_ffn_w2': _L0_ffn_in['w2'], 'L0_ffn_mean_w2': _L0_ffn_in['mean_w2'], 'L0_ffn_w3': _L0_ffn_in['w3'], 'L0_ffn_mean_w3': _L0_ffn_in['mean_w3']}
    _x0 = _d['L0_attn_inputs']
    _d['L0_attn_inputs'] = jax.random.normal(jax.random.fold_in(jax.random.key(seed), 1), (4, 256, 512), dtype=_x0.dtype)
    del _x0
    return _d

def reference(L0_attn_inputs, L0_attn_conv_w, L0_attn_conv_b, L0_attn_wq, L0_attn_bq, L0_attn_wk, L0_attn_bk, L0_attn_wv, L0_attn_bv, L0_attn_wo, L0_attn_bo, L0_attn_proj_w, L0_attn_proj_b, L0_ffn_w1, L0_ffn_mean_w1, L0_ffn_w2, L0_ffn_mean_w2, L0_ffn_w3, L0_ffn_mean_w3):

    def _L0_attn_ref(inputs, conv_w, conv_b, wq, bq, wk, bk, wv, bv, wo, bo, proj_w, proj_b):
        import jax, jax.numpy as jnp
        import numpy as np
        from jax import lax
        BLOCK_LEN = 128
        NEG_INF = -1000000000.0
        N, L, Dm = inputs.shape
        x = lax.conv_general_dilated(inputs, conv_w, window_strides=(1,), padding='SAME', dimension_numbers=('NWC', 'WIO', 'NWC')) + conv_b
        q, k, v = jnp.split(x, 3, axis=-1)
        W_ = q.shape[-1]
        nb = L // BLOCK_LEN
        q = q.reshape(N * nb, BLOCK_LEN, W_)
        k = k.reshape(N * nb, BLOCK_LEN, W_)
        v = v.reshape(N * nb, BLOCK_LEN, W_)
        dh = wq.shape[-1]
        qh = jnp.einsum('btd,dhe->bthe', q, wq) + bq
        kh = jnp.einsum('btd,dhe->bthe', k, wk) + bk
        vh = jnp.einsum('btd,dhe->bthe', v, wv) + bv
        scale = 1.0 / jnp.sqrt(jnp.asarray(dh, qh.dtype))
        scores = jnp.einsum('bqhe,bkhe->bhqk', qh * scale, kh)
        causal = jnp.tril(jnp.ones((BLOCK_LEN, BLOCK_LEN), bool))
        scores = jnp.where(causal, scores, NEG_INF)
        p = jax.nn.softmax(scores, axis=-1)
        o = jnp.einsum('bhqk,bkhe->bqhe', p, vh)
        o = jnp.einsum('bqhe,hed->bqd', o, wo) + bo
        o = o.reshape(N, L, W_)
        return o @ proj_w + proj_b

    def _L0_ffn_ref(hidden_states, w1, mean_w1, w2, mean_w2, w3, mean_w3):
        import jax, jax.numpy as jnp
        import numpy as np
        HID, INTER = (512, 1792)
        B, S = (2, 256)

        def _binary_diff_weight(w, base):
            d = w - base
            coeff = jnp.mean(jnp.abs(d))
            return base + coeff * jnp.sign(d)
        W1 = _binary_diff_weight(w1, mean_w1)
        W2 = _binary_diff_weight(w2, mean_w2)
        W3 = _binary_diff_weight(w3, mean_w3)
        gate = jnp.einsum('bsh,ih->bsi', hidden_states, W1)
        up = jnp.einsum('bsh,ih->bsi', hidden_states, W3)
        h = jax.nn.silu(gate) * up
        return jnp.einsum('bsi,hi->bsh', h, W2)
    x = L0_attn_inputs
    x = x + 0.5 * _L0_ffn_ref(_layernorm(x, axis=-1), L0_ffn_w1, L0_ffn_mean_w1, L0_ffn_w2, L0_ffn_mean_w2, L0_ffn_w3, L0_ffn_mean_w3)
    x = x + _L0_attn_ref(_layernorm(x, axis=-1), L0_attn_conv_w, L0_attn_conv_b, L0_attn_wq, L0_attn_bq, L0_attn_wk, L0_attn_bk, L0_attn_wv, L0_attn_bv, L0_attn_wo, L0_attn_bo, L0_attn_proj_w, L0_attn_proj_b)
    x = x + 0.5 * _L0_ffn_ref(_layernorm(x, axis=-1), L0_ffn_w1, L0_ffn_mean_w1, L0_ffn_w2, L0_ffn_mean_w2, L0_ffn_w3, L0_ffn_mean_w3)
    return x

_drawn_inputs = setup_inputs


def setup_inputs(seed=0):
    import zlib

    import numpy as np

    out = dict(_drawn_inputs(seed))
    spreads = {'L0_attn_conv_b': (0.0, 0.1),
     'L0_attn_bq': (0.0, 0.411),
     'L0_attn_bk': (0.0, 0.8),
     'L0_attn_bv': (0.0, 0.1),
     'L0_attn_bo': (0.0, 0.1),
     'L0_attn_proj_b': (0.0, 0.1)}
    factors = {}
    for name, (base, spread) in spreads.items():
        noise = np.random.default_rng([zlib.crc32(name.encode()), seed]).standard_normal(out[name].shape)
        drawn = base * np.exp(spread * noise) if base else spread * noise
        out[name] = jnp.asarray(drawn.astype(out[name].dtype))
    for name, factor in factors.items():
        out[name] = (out[name] * factor).astype(out[name].dtype)
    return out
```

```python
from contextlib import ExitStack

import concourse.bass as bass
from concourse import mybir

F32 = mybir.dt.float32
F32R = mybir.dt.float32r
I32 = mybir.dt.int32
I8 = mybir.dt.int8
ALU = mybir.AluOpType
ACT = mybir.ActivationFunctionType
AX_X = mybir.AxisListType.X

P = 128
BANK = 512
TOK = 1024
DM = 512
INTER = 1792
SEQS = 4
SEQ = TOK // SEQS
HALF = 512
KT = DM // P
NT = INTER // P
HT = HALF // P
W = 128
HEADS = 16
DH = 64
HD = HEADS * DH
BLK = 128
TAPS = 3
NEG = -1e30
EPS = 1e-5
RSQRT_MAGIC = float(0x5F3759DF)
RING = 4
CH1 = NT // 2
PREFETCH = 4
SCALE = DH ** -0.5
CONV_OUT = 3 * W
AW = TAPS * KT * CONV_OUT // BANK + 2 * HD // BANK
BW = 2 * HD // BANK + DM // BANK
ST = SEQ // P
MT = HD // P
GH = 8
UNITS = ST * HEADS // GH
B_CONV, B_Q, B_K, B_V, B_O = 0, 3, 3 + MT, 3 + 2 * MT, 3 + 3 * MT
F_Q, F_K, F_V, F_S, F_OUT, FILLS = 2, 6, 10, 14, 22, 24
T_FILLS = 2 + 3 * UNITS
LINKS = 20 + 2 * UNITS


def at_least(eng, sem, value):
    if not (isinstance(value, int) and value <= 0):
        eng.wait_ge(sem, value)


def macaron(nc, x_in, w1_in, base1_in, w23_in, base23_in, attw_in, bias_in, projb_in, scratch, out):
    with ExitStack() as ctx:
        def at(name, shape, offset, dt=F32):
            return nc.alloc_sbuf_tensor_at(name, [P] + shape, dt, offset=offset)

        def sem(name):
            return ctx.enter_context(nc.semaphore(name))

        COMMON = 640
        x = at("x", [TOK // P, DM], COMMON)
        o = COMMON + 4 * TOK // P * DM
        ident = at("ident", [P], o)
        ones = at("ones", [P], o + 512)
        stats = at("stats", [HT, 6], o + 1024)
        mv = at("mv", [HT, 2], o + 1120)
        rstd = at("rstd", [HT], o + 1152)
        newton = at("newton", [HT], o + 1184)
        varep = at("varep", [HT], o + 1216)
        abs_sum = at("abs_sum", [3, NT], o + 1248)
        abs_tot = at("abs_tot", [3], o + 1440)
        coeff = at("coeff", [3], o + 1472)
        ident_r = at("ident_r", [P], o + 1536, F32R)
        mask_r = at("mask_r", [4, BLK], o + 2048, F32R)
        projb = at("projb", [DM], o + 4096)
        bias = at("bias", [B_O + 1], o + 6144)
        o = COMMON + 22656
        w13_h = at("w13_h", [2, 2, 512], o, F32R)
        w13_l = at("w13_l", [2, 2, 512], o + 8192, F32R)
        w2_h = at("w2_h", [2, DM], o + 16384, F32R)
        w2_l = at("w2_l", [2, DM], o + 20480, F32R)
        hid = at("hid", [2, HALF], o + 24576)
        hid_h = at("hid_h", [2, HALF], o + 28672, F32R)
        hid_l = at("hid_l", [2, HALF], o + 32768, F32R)
        xT_h = at("xT_h", [KT, HALF], o + 36864, F32R)
        xT_l = at("xT_l", [KT, HALF], o + 45056, F32R)
        WTS = o + 53248
        wts = at("wts", [NT, 3, 512], WTS)
        R3 = WTS + 4 * NT * 3 * 512
        sgn = at("sgn", [3, NT, 512], R3, I8)
        gates = at("gates", [NT, HALF], R3 + 21504)
        raw = at("raw", [RING, 1024], R3 + 50176)
        xn = [at("xn_a", [HT, DM], R3 + 21504), at("xn_b", [HT, DM], R3 + 57344)]

        mask_f = at("mask_f", [4, BLK], R3 + 21504 + 4 * 512 * (NT - 1))

        aw_h = at("aw_h", [AW, BANK], R3, F32R)
        aw_l = at("aw_l", [AW, BANK], R3 + 26624, F32R)
        aw_raw = at("aw_raw", [2, BANK], R3 + 53248)
        a = COMMON + 22656
        bw_h = at("bw_h", [BW, BANK], a, F32R)
        bw_l = at("bw_l", [BW, BANK], a + 10240, F32R)
        qT_h = at("qT_h", [MT, SEQ], a + 20480, F32R)
        qT_l = at("qT_l", [MT, SEQ], a + 28672, F32R)
        kT_h = at("kT_h", [MT, SEQ], a + 36864, F32R)
        kT_l = at("kT_l", [MT, SEQ], a + 45056, F32R)
        a = WTS + PREFETCH * 6144
        xp_h = at("xp_h", [KT, SEQ + 2], a, F32R)
        xp_l = at("xp_l", [KT, SEQ + 2], a + 4128, F32R)
        cT_h = at("cT_h", [3, SEQ], a + 8256, F32R)
        cT_l = at("cT_l", [3, SEQ], a + 11328, F32R)
        v_h = at("v_h", [ST, HD], a + 14400, F32R)
        v_l = at("v_l", [ST, HD], a + 22592, F32R)
        probs = at("probs", [2, 2, 4 * BLK], a + 30784)
        pT_h = at("pT_h", [2, 4 * BLK], a + 38976, F32R)
        pT_l = at("pT_l", [2, 4 * BLK], a + 43072, F32R)
        heads = at("heads", [2, GH * DH], a + 47168)
        hT_h = at("hT_h", [4, P], a + 51264, F32R)
        hT_l = at("hT_l", [4, P], a + 53312, F32R)
        yT_h = at("yT_h", [SEQ], a + 55360, F32R)
        yT_l = at("yT_l", [SEQ], a + 56384, F32R)
        row_max = at("row_max", [2, GH], a + 57408)
        neg_max = at("neg_max", [2, GH], a + 57472)
        row_sum = at("row_sum", [2, GH], a + 57536)
        inv_sum = at("inv_sum", [2, GH], a + 57600)
        out_bias = at("out_bias", [1], a + 57664)
        xs = at("xs", [ST, DM], R3 + 57344)

        def turn_of(u, what):
            order = []
            for v in range(UNITS):
                order += [(v, 0), (v, 1)] + ([(v - 1, 2)] if v else [])
            return (order + [(UNITS - 1, 2)]).index((u, what))

        def columns(part, first, n):
            return part[:, :, :].rearrange("p c n -> p (c n)")[:, first:first + n]

        def conv_w(part, tap, k, m):
            return columns(part, (tap * KT + k) * CONV_OUT + m * W, W)

        K_COL = TAPS * KT * CONV_OUT
        Q_COL = K_COL + HD
        V_COL, O_COL, PROJ_COL = 0, HD, 2 * HD

        bank = [ctx.enter_context(nc.psum_tensor(f"bank{i}", [P, BANK], F32)) for i in range(8)]
        ps_gate, ps_up, acc = bank[0:2], bank[2:4], bank[4:8]
        ps_xT = bank[0:4]
        ps_share, ps_turn, ps_heads, ps_y = bank[0:4], bank[4:6], bank[6], bank[7]

        x_loaded = [sem("x_loaded_a"), sem("x_loaded_b")]
        raw_loaded = [sem(f"raw_loaded{i}") for i in range(RING)]
        diff_done = sem("diff_done")
        sign_done = sem("sign_done")
        abs_done = sem("abs_done")
        tot_ready = sem("tot_ready")
        tot_sum = sem("tot_sum")
        coeff_ready = sem("coeff_ready")
        const_ready = sem("const_ready")
        dve_chain = sem("dve_chain")
        xn_ready = sem("xn_ready")
        xT_done = sem("xT_done")
        xT_hi = sem("xT_hi")
        xT_lo = sem("xT_lo")
        w1_formed = sem("w1_formed")
        w3_formed = sem("w3_formed")
        w2_formed = sem("w2_formed")
        w13_hi = sem("w13_hi")
        w13_lo = sem("w13_lo")
        w2_hi = sem("w2_hi")
        w2_lo = sem("w2_lo")
        gate_done = sem("gate_done")
        up_done = sem("up_done")
        down_done = sem("down_done")
        silu_done = sem("silu_done")
        hid_ready = sem("hid_ready")
        hid_hi = sem("hid_hi")
        hid_lo = sem("hid_lo")
        x_updated = sem("x_updated")
        w_saved = sem("w_saved")
        w_loaded = [sem("w_loaded_even"), sem("w_loaded_odd")]
        stored = sem("stored")
        small_loaded = sem("small_loaded")
        mask_ready = sem("mask_ready")
        consts_r = sem("consts_r")
        pads_ready = sem("pads_ready")
        aw_loaded = [sem("aw_loaded_even"), sem("aw_loaded_odd")]
        aw_hi = sem("aw_hi")
        aw_lo = sem("aw_lo")
        bias_sum = sem("bias_sum")
        bias_ready = sem("bias_ready")
        att_chain = sem("att_chain")
        xs_ready = sem("xs_ready")
        fill_done = sem("fill_done")
        fill_hi = sem("fill_hi")
        fill_lo = sem("fill_lo")
        turn_done = sem("turn_done")
        turn_hi = sem("turn_hi")
        turn_lo = sem("turn_lo")
        max_ready = sem("max_ready")
        exp_done = sem("exp_done")
        pv_done = sem("pv_done")
        heads_ready = sem("heads_ready")
        wo_done = sem("wo_done")
        y_hi = sem("y_hi")
        y_lo = sem("y_lo")
        x_attended = sem("x_attended")

        def chunk_slot(k):
            return k % RING, k // RING + 1

        block = ctx.enter_context(nc.Block())

        @block.sync
        def _(sp):
            def load_chunk1(k):
                at_least(sp, abs_done, k - RING + 1)
                at_least(sp, sign_done, k - RING + 1)
                slot, _ = chunk_slot(k)
                sp.dma_start(raw[:, slot, :], w1_in[:, 1024 * k:1024 * (k + 1)]).then_inc(raw_loaded[slot], 16)
                sp.dma_start(wts[:, 2 * k:2 * k + 2, 0, :],
                             base1_in[:, 1024 * k:1024 * (k + 1)].rearrange("p (t n) -> p t n", t=2)
                             ).then_inc(raw_loaded[slot], 16)

            def load_chunk23(t, slot):
                at_least(sp, abs_done, t + (CH1 - RING + 1))
                at_least(sp, sign_done, t + (CH1 - RING + 1))
                sp.dma_start(raw[:, slot, :], w23_in[:, bass.ds(t * 1024, 1024)]).then_inc(raw_loaded[slot], 16)
                sp.dma_start(wts[:, bass.ds(t, 1), 1:3, :].rearrange("p a b n -> p (a b) n"),
                             base23_in[:, bass.ds(t * 1024, 1024)].rearrange("p (t n) -> p t n", t=2)
                             ).then_inc(raw_loaded[slot], 16)

            def load_attw_chunk(c, slot):
                if isinstance(c, int) and c == AW + HD // BANK + 2:
                    sp.wait_ge(bias_sum, 1)
                at_least(sp, aw_hi, c - 1)
                at_least(sp, aw_lo, c - 1)
                sp.dma_start(aw_raw[:, slot, :], attw_in[:, bass.ds(c * BANK, BANK)]).then_inc(aw_loaded[slot], 16)

            def load_attw(c0, c1, first):
                if first:
                    sp.wait_ge(abs_done, CH1 + NT)
                    sp.wait_ge(sign_done, CH1 + NT)
                for c in range(c0, c0 + 2):
                    load_attw_chunk(c, c % 2)
                with sp.Fori(1, (c1 - c0) // 2) as j:
                    for q in range(2):
                        load_attw_chunk(j * 2 + (c0 + q), (c0 + q) % 2)
                if (c1 - c0) % 2:
                    load_attw_chunk(c1 - 1, (c1 - 1) % 2)

            def load_formed(i, slot, j):
                at_least(sp, w_loaded[slot], j * 16)
                sp.dma_start(wts[:, bass.ds(i, 1), :, :].rearrange("p a b n -> p (a b n)"),
                             scratch[:, bass.ds(i * 1536, 1536)]).then_inc(w_loaded[slot], 16)

            for k in range(2):
                load_chunk1(k)
            xv = x_in.rearrange("(t p) d -> p t d", p=P)
            sp.dma_start(x[:, 0:HT, :], xv[:, 0:HT, :]).then_inc(x_loaded[0], 16)
            sp.dma_start(bias[:, :], bias_in).then_inc(small_loaded, 16)
            sp.dma_start(projb[:, :], projb_in.partition_broadcast(P)).then_inc(small_loaded, 16)
            for k in range(2, CH1):
                load_chunk1(k)
            for t in range(2):
                load_chunk23(t, chunk_slot(CH1 + t)[0])
            with sp.Fori(0, (NT - 2) // 4) as j:
                for q in range(4):
                    load_chunk23(j * 4 + (2 + q), chunk_slot(CH1 + 2 + q)[0])
            sp.dma_start(x[:, HT:2 * HT, :], xv[:, HT:2 * HT, :]).then_inc(x_loaded[1], 16)
            with sp.Fori(0, NT) as i:
                sp.wait_ge(w2_formed, i + 1)
                sp.dma_start(scratch[:, bass.ds(i * 1536, 1536)],
                             wts[:, bass.ds(i, 1), :, :].rearrange("p a b n -> p (a b n)")).then_inc(w_saved, 16)
            load_attw(0, AW, True)
            sp.wait_ge(w_saved, 16 * NT)
            load_attw(AW, AW + BW, False)
            sp.wait_ge(w2_lo, 2 * NT)
            for i in range(PREFETCH):
                load_formed(i, i % 2, i // 2)
            sp.wait_ge(x_attended, 2 * HT)
            with sp.Fori(PREFETCH // 2, NT // 2) as j:
                for q in range(2):
                    load_formed(j * 2 + q, q, j)
            for t in range(2 * HT):
                sp.wait_ge(x_updated, 2 * HT + t + 1)
                sp.dma_start(out[t * P:(t + 1) * P, :], x[:, t, :]).then_inc(stored, 16)
            sp.wait_ge(stored, 16 * 2 * HT)

        @block.gpsimd
        def _(pool):
            pool.memset(ident[:, :], 0.0).then_inc(const_ready, 1)
            pool.memset(ones[:, :], 1.0).then_inc(const_ready, 1)
            pool.wait_ge(const_ready, 2)
            pool.affine_select(out=ident[:, :], in_=ident[:, :], compare_op=ALU.not_equal, fill=1.0,
                               base=0, pattern=[[-1, P]], channel_multiplier=1).then_inc(const_ready, 1)
            pool.memset(mask_f[:, :, :], 0.0).then_inc(mask_ready, 1)
            pool.wait_ge(mask_ready, 1)
            pool.affine_select(out=mask_f[:, :, :], in_=mask_f[:, :, :], compare_op=ALU.is_ge, fill=NEG,
                               base=0, pattern=[[0, 4], [-1, BLK]], channel_multiplier=1).then_inc(mask_ready, 1)

            def diff1(k):
                slot, use = chunk_slot(k)
                pool.wait_ge(raw_loaded[slot], 32 * use)
                r = raw[:, slot, :].rearrange("p (t n) -> p t n", t=2)
                pool.tensor_tensor(r, r, wts[:, 2 * k:2 * k + 2, 0, :], ALU.subtract).then_inc(diff_done, 1)

            def diff23(t, slot, use):
                pool.wait_ge(raw_loaded[slot], use * 32)
                pool.tensor_tensor(raw[:, slot, :], raw[:, slot, :],
                                   wts[:, bass.ds(t, 1), 1:3, :].rearrange("p a b n -> p (a b n)"),
                                   ALU.subtract).then_inc(diff_done, 1)

            for k in range(CH1):
                diff1(k)
            for t in range(2):
                diff23(t, *chunk_slot(CH1 + t))
            with pool.Fori(0, (NT - 2) // 4) as j:
                for q in range(4):
                    slot, use = chunk_slot(CH1 + 2 + q)
                    diff23(j * 4 + (2 + q), slot, j + use)

        @block.scalar
        def _(act):
            def sign1(k):
                act.wait_ge(diff_done, k + 1)
                slot, _ = chunk_slot(k)
                act.activation(sgn[:, 0, 2 * k:2 * k + 2, :],
                               raw[:, slot, :].rearrange("p (t n) -> p t n", t=2), ACT.Sign).then_inc(sign_done, 1)

            def sign23(t, slot):
                act.wait_ge(diff_done, t + (CH1 + 1))
                act.activation(sgn[:, 1:3, bass.ds(t, 1), :].rearrange("p a b n -> p a (b n)"),
                               raw[:, slot, :].rearrange("p (t n) -> p t n", t=2), ACT.Sign).then_inc(sign_done, 1)

            def xT_high(p):
                for k in range(KT):
                    act.wait_ge(xT_done, KT * p + k + 1)
                    act.activation(xT_h[:, k, :], ps_xT[k][:, :], ACT.Copy).then_inc(xT_hi, 1)

            def w1_high(t, b):
                act.wait_ge(w1_formed, t + 1)
                at_least(act, gate_done, t - 1)
                act.activation(w13_h[:, b, 0, :], wts[:, bass.ds(t, 1), 0, :].rearrange("p a n -> p (a n)"),
                               ACT.Copy).then_inc(w13_hi, 1)

            def silu_store(t, b):
                act.wait_ge(gate_done, t + 1)
                act.activation(gates[:, bass.ds(t, 1), :].rearrange("p a n -> p (a n)"), ps_gate[b][:, :],
                               ACT.Silu).then_inc(silu_done, 1)

            def w13_high(i, base, b, first):
                if first:
                    act.wait_ge(w3_formed, i + 1)
                at_least(act, up_done, i + (base - 1))
                src = wts[:, bass.ds(i, 1), 1 if first else 0:2, :].rearrange("p a b n -> p (a b) n")
                act.activation(w13_h[:, b, 1 if first else 0:2, :], src, ACT.Copy).then_inc(w13_hi, 1)

            def w2_high(i, base, b, first):
                if first:
                    act.wait_ge(w2_formed, i + 1)
                at_least(act, down_done, i + (base - 1))
                act.activation(w2_h[:, b, :], wts[:, bass.ds(i, 1), 2, :].rearrange("p a n -> p (a n)"),
                               ACT.Copy).then_inc(w2_hi, 1)

            def hid_high(i, base, b, first):
                act.wait_ge(hid_ready, i + (base + 1))
                at_least(act, down_done, i + (base - 1))
                src = gates[:, bass.ds(i, 1), :].rearrange("p a n -> p (a n)") if first else hid[:, b, :]
                act.activation(hid_h[:, b, :], src, ACT.Copy).then_inc(hid_hi, 1)

            def silu(i, base, b):
                act.wait_ge(gate_done, i + (base + 1))
                at_least(act, hid_lo, i + (base - 1))
                act.activation(hid[:, b, :], ps_gate[b][:, :], ACT.Silu).then_inc(silu_done, 1)

            def attw_high(c, slot, use):
                act.wait_ge(aw_loaded[slot], use * 16)
                part, at_c = (bw_h, c - AW) if isinstance(c, int) and c >= AW else (aw_h, c)
                act.activation(part[:, bass.ds(at_c, 1), :].rearrange("p a n -> p (a n)"), aw_raw[:, slot, :],
                               ACT.Copy).then_inc(aw_hi, 1)

            def step(i, base, b, first, pair):
                if base == 2 * NT:
                    act.wait_ge(w_loaded[b], pair * 16 + 16)
                if base == NT:
                    attw_high(i - 1, 1 - b, pair + b)
                w13_high(i, base, b, first)
                if not first:
                    silu(i - 1, base, 1 - b)
                hid_high(i - 1, base, 1 - b, first)
                w2_high(i, base, b, first)

            def passes(p, carry_on):
                base, first = NT * p, p == 0
                step(1, base, 1, first, 0)
                with act.Fori(1, NT // 2) as j:
                    step(j * 2, base, 0, first, j)
                    step(j * 2 + 1, base, 1, first, j)
                if carry_on:
                    w13_high(0, base + NT, 0, False)
                if not first:
                    silu(NT - 1, base, 1)
                hid_high(NT - 1, base, 1, first)
                if carry_on:
                    w2_high(0, base + NT, 0, False)
                    xT_high(p + 1)

            act.wait_ge(const_ready, 3)
            act.activation(ident_r[:, :], ident[:, :], ACT.Copy).then_inc(consts_r, 1)
            act.wait_ge(mask_ready, 2)
            act.activation(mask_r[:, :, :], mask_f[:, :, :], ACT.Copy).then_inc(consts_r, 1)
            for k in range(CH1):
                sign1(k)
            xT_high(0)
            w1_high(0, 0)
            w1_high(1, 1)
            silu_store(0, 0)
            sign23(0, chunk_slot(CH1)[0])
            with act.Fori(0, (NT - 2) // 4) as j:
                for q in range(4):
                    t = j * 4 + (2 + q)
                    w1_high(t, q % 2)
                    silu_store(t - 1, 1 - q % 2)
                    sign23(t - 1, chunk_slot(CH1 + 1 + q)[0])
            silu_store(NT - 1, 1)
            sign23(NT - 1, chunk_slot(CH1 + NT - 1)[0])
            w13_high(0, 0, 0, True)
            w2_high(0, 0, 0, True)
            passes(0, True)
            act.wait_ge(hid_lo, NT)
            passes(1, False)

            act.wait_ge(down_done, 2 * NT)
            for c in range(AW, AW + BW):
                attw_high(c, c % 2, c // 2 + 1)

            def high(out, in_, bias_column=None):
                if bias_column is None:
                    return act.activation(out, in_, ACT.Copy)
                return act.activation(out, in_, ACT.Identity, bias=bias_column)

            with act.Fori(0, SEQS) as s:
                def turned(t):
                    act.wait_ge(turn_done, s * T_FILLS + (t + 1))
                    return ps_turn[t % 2]

                def filled(f):
                    act.wait_ge(fill_done, s * FILLS + (f + 1))
                    return ps_share[f % 4]

                for t in range(2):
                    high(xp_h[:, 2 * t:2 * t + 2, 1:SEQ + 1],
                         turned(t)[:, :].rearrange("p (k n) -> p k n", k=2)).then_inc(turn_hi, 1)
                for m in range(3):
                    src = filled(m // 2)[:, m % 2 * SEQ:(m % 2 + 1) * SEQ]
                    ins = high(cT_h[:, m, :], src, bias[:, B_CONV + m:B_CONV + m + 1])
                    if m:
                        ins.then_inc(fill_hi, 1)
                for f, part, col in ([(F_Q + n, qT_h, B_Q) for n in range(4)] + [(F_K + n, kT_h, B_K) for n in range(4)]):
                    src = filled(f)
                    for e in range(2):
                        m = (f - F_Q) % 4 * 2 + e
                        ins = high(part[:, m, :], src[:, e * SEQ:(e + 1) * SEQ], bias[:, col + m:col + m + 1])
                    ins.then_inc(fill_hi, 1)
                for n in range(2 * ST):
                    high(v_h[:, n // 2, n % 2 * BANK:(n % 2 + 1) * BANK], filled(F_V + n)[:, :]).then_inc(fill_hi, 1)

                def exps(u):
                    act.wait_ge(max_ready, s * UNITS + (u + 1))
                    if u >= 2:
                        act.wait_ge(turn_done, s * T_FILLS + (2 + turn_of(u - 2, 1) + 1))
                        act.wait_ge(heads_ready, s * UNITS + (u - 1))
                    for e in range(2):
                        src = ps_share[(F_S + 2 * u + e) % 4]
                        for k in range(4):
                            ins = act.activation(probs[:, u % 2, e, k * BLK:(k + 1) * BLK],
                                                 src[:, k * BLK:(k + 1) * BLK], ACT.Exp,
                                                 bias=neg_max[:, u % 2, 4 * e + k:4 * e + k + 1], scale=SCALE,
                                                 accum_out=row_sum[:, u % 2, 2 * k + e:2 * k + e + 1])
                        ins.then_inc(exp_done, 1)

                def probs_high(u):
                    if u:
                        act.wait_ge(pv_done, s * UNITS + u)
                    for e in range(2):
                        high(pT_h[:, e, :], turned(2 + turn_of(u, e))[:, :]).then_inc(turn_hi, 1)

                def heads_high(u):
                    if u:
                        act.wait_ge(wo_done, s * UNITS + u)
                    high(hT_h[:, :, :].rearrange("p a n -> p (a n)"), turned(2 + turn_of(u, 2))[:, :]).then_inc(turn_hi, 1)

                exps(0)
                for u in range(UNITS):
                    probs_high(u)
                    if u:
                        heads_high(u - 1)
                    if u + 1 < UNITS:
                        exps(u + 1)
                heads_high(UNITS - 1)
                act.wait_ge(wo_done, s * UNITS + UNITS)
                act.wait_ge(bias_ready, 1)
                high(yT_h[:, :], ps_y[:, 0:SEQ], out_bias[:, :]).then_inc(y_hi, 1)

            act.wait_ge(x_attended, 2 * HT)
            act.wait_ge(w_loaded[0], 16)
            xT_high(2)
            w13_high(0, 2 * NT, 0, False)
            w2_high(0, 2 * NT, 0, False)
            passes(2, True)
            passes(3, False)

        @block.vector
        def _(dve):
            chain = [0]

            def link(ins):
                chain[0] += 1
                ins.then_inc(dve_chain, 1)
                dve.wait_ge(dve_chain, chain[0])

            def layer_norm(tiles, target, link, ready):
                n = len(tiles)
                for t in range(n):
                    last = dve.bn_stats(stats[:, t, :], tiles[t])
                link(last)
                v, r, w = varep[:, 0:n], rstd[:, 0:n], newton[:, 0:n]
                dve.memset(v, EPS)
                for t in range(n):
                    last = dve.bn_aggr(mv[:, t, :], stats[:, t, :])
                link(last)
                link(dve.tensor_tensor(v, mv[:, 0:n, 1], v, ALU.add))
                link(dve.tensor_scalar(r.bitcast(I32), v.bitcast(I32), -0.5, RSQRT_MAGIC, ALU.mult, ALU.add))
                for _ in range(4):
                    link(dve.tensor_tensor(w, r, r, ALU.mult))
                    link(dve.tensor_tensor(w, w, v, ALU.mult))
                    link(dve.tensor_scalar(w, w, -0.5, 1.5, ALU.mult, ALU.add))
                    link(dve.tensor_tensor(r, r, w, ALU.mult))
                for t in range(n):
                    last = dve.tensor_scalar(target[:, t, :], tiles[t], mv[:, t, 0:1], rstd[:, t:t + 1],
                                             ALU.subtract, ALU.mult)
                last.then_inc(ready, 1)

            def xT_low(p):
                for k in range(KT):
                    dve.wait_ge(xT_hi, KT * p + k + 1)
                    dve.tensor_tensor(xT_l[:, k, :], ps_xT[k][:, :], xT_h[:, k, :].bitcast(F32),
                                      ALU.subtract).then_inc(xT_lo, 1)

            def sum_abs1(k):
                dve.wait_ge(diff_done, k + 1)
                dve.tensor_reduce(abs_sum[:, 0, k:k + 1], raw[:, chunk_slot(k)[0], :], AX_X, ALU.add,
                                  apply_absolute_value=True).then_inc(abs_done, 1)

            def sum_abs23(t, slot):
                dve.wait_ge(diff_done, t + (CH1 + 1))
                dve.tensor_reduce(abs_sum[:, 1:3, bass.ds(t, 1)].rearrange("p a b -> p (a b)"),
                                  raw[:, slot, :].rearrange("p (a n) -> p a n", a=2),
                                  AX_X, ALU.add, apply_absolute_value=True).then_inc(abs_done, 1)

            def form(m, i, done):
                place = wts[:, bass.ds(i, 1), m, :].rearrange("p a n -> p (a n)")
                dve.scalar_tensor_tensor(out=place, in0=sgn[:, m, bass.ds(i, 1), :].rearrange("p a n -> p (a n)"),
                                         scalar=coeff[:, m:m + 1], in1=place, op0=ALU.mult,
                                         op1=ALU.add).then_inc(done, 1)

            def w1_low(t, b):
                dve.wait_ge(w13_hi, t + 1)
                at_least(dve, gate_done, t - 1)
                dve.tensor_tensor(w13_l[:, b, 0, :], wts[:, bass.ds(t, 1), 0, :].rearrange("p a n -> p (a n)"),
                                  w13_h[:, b, 0, :].bitcast(F32), ALU.subtract).then_inc(w13_lo, 1)

            def w13_low(i, base, b, first):
                dve.wait_ge(w13_hi, i + (base + NT + 1))
                lo = 1 if first else 0
                src = wts[:, bass.ds(i, 1), lo:2, :].rearrange("p a b n -> p (a b) n")
                dve.tensor_tensor(w13_l[:, b, lo:2, :], src, w13_h[:, b, lo:2, :].bitcast(F32),
                                  ALU.subtract).then_inc(w13_lo, 1)

            def w2_low(i, base, b):
                dve.wait_ge(w2_hi, i + (base + 1))
                dve.tensor_tensor(w2_l[:, b, :], wts[:, bass.ds(i, 1), 2, :].rearrange("p a n -> p (a n)"),
                                  w2_h[:, b, :].bitcast(F32), ALU.subtract).then_inc(w2_lo, 1)

            def hidden(i, base, b, first):
                dve.wait_ge(silu_done, i + (base + 1))
                dve.wait_ge(up_done, i + (base + 1))
                h = gates[:, bass.ds(i, 1), :].rearrange("p a n -> p (a n)") if first else hid[:, b, :]
                dve.tensor_tensor(h, h, ps_up[b][:, :], ALU.mult).then_inc(hid_ready, 1)
                dve.wait_ge(hid_hi, i + (base + 1))
                dve.tensor_tensor(hid_l[:, b, :], h, hid_h[:, b, :].bitcast(F32), ALU.subtract).then_inc(hid_lo, 1)

            def attw_low(c, slot):
                dve.wait_ge(aw_hi, c + 1)
                late = isinstance(c, int) and c >= AW
                high, low, at_c = (bw_h, bw_l, c - AW) if late else (aw_h, aw_l, c)
                high, low = (v[:, bass.ds(at_c, 1), :].rearrange("p a n -> p (a n)") for v in (high, low))
                dve.tensor_tensor(low, aw_raw[:, slot, :], high.bitcast(F32), ALU.subtract).then_inc(aw_lo, 1)

            def step(i, base, b, first):
                if base == NT:
                    attw_low(i - 1, 1 - b)
                if first:
                    form(1, i, w3_formed)
                    form(2, i, w2_formed)
                w13_low(i, base, b, first)
                hidden(i - 1, base, 1 - b, first)
                w2_low(i, base, b)

            def passes(p, carry_on):
                base, first = NT * p, p == 0
                step(1, base, 1, first)
                with dve.Fori(1, NT // 2) as j:
                    step(j * 2, base, 0, first)
                    step(j * 2 + 1, base, 1, first)
                if carry_on:
                    w13_low(0, base + NT, 0, False)
                hidden(NT - 1, base, 1, first)
                if carry_on:
                    w2_low(0, base + NT, 0)
                    xT_low(p + 1)
                dve.wait_ge(down_done, base + NT)
                for t in range(HT):
                    tile = x[:, HT * p % (2 * HT) + t, :]
                    dve.scalar_tensor_tensor(out=tile, in0=acc[t][:, :], scalar=0.5, in1=tile, op0=ALU.mult,
                                             op1=ALU.add).then_inc(x_updated, 1)

            def total(m, n):
                dve.tensor_reduce(abs_tot[:, m:m + 1], abs_sum[:, m, 0:n], AX_X, ALU.add).then_inc(tot_ready, 1)

            def mean(m, col):
                link(dve.tensor_scalar(coeff[:, m:m + 1], ps_up[0][:, col:col + 1], 1.0 / (INTER * DM), None, ALU.mult))

            for k in range(CH1):
                sum_abs1(k)
                if k == 2:
                    dve.wait_ge(x_loaded[0], 16)
                    layer_norm([x[:, t, :] for t in range(HT)], xn[0], link, xn_ready)
            xT_low(0)
            dve.wait_ge(abs_done, CH1)
            total(0, CH1)
            dve.wait_ge(tot_sum, 1)
            dve.wait_ge(sign_done, CH1)
            mean(0, 0)
            form(0, 0, w1_formed)
            w1_low(0, 0)
            form(0, 1, w1_formed)
            w1_low(1, 1)
            sum_abs23(0, chunk_slot(CH1)[0])
            with dve.Fori(0, (NT - 2) // 4) as j:
                for q in range(4):
                    t = j * 4 + (2 + q)
                    form(0, t, w1_formed)
                    w1_low(t, q % 2)
                    sum_abs23(t - 1, chunk_slot(CH1 + 1 + q)[0])
            sum_abs23(NT - 1, chunk_slot(CH1 + NT - 1)[0])
            dve.wait_ge(abs_done, CH1 + NT)
            total(1, NT)
            total(2, NT)
            dve.wait_ge(x_loaded[1], 16)
            dve.wait_ge(tot_sum, 2)
            dve.wait_ge(sign_done, CH1 + NT)
            mean(1, 1)
            mean(2, 2)
            form(1, 0, w3_formed)
            form(2, 0, w2_formed)
            w13_low(0, 0, 0, True)
            w2_low(0, 0, 0)
            layer_norm([x[:, HT + t, :] for t in range(HT)], xn[1], link, xn_ready)
            passes(0, True)
            passes(1, False)

            for part in (xp_h, xp_l):
                for column in (0, SEQ + 1):
                    ins = dve.memset(part[:, :, column:column + 1].bitcast(F32), 0.0)
            ins.then_inc(pads_ready, 1)
            for c in range(AW, AW + BW):
                attw_low(c, c % 2)
            dve.wait_ge(small_loaded, 32)
            dve.wait_ge(bias_sum, 2)
            dve.tensor_tensor(out_bias[:, :], ps_y[:, 0:1], bias[:, B_O:B_O + 1], ALU.add).then_inc(bias_ready, 1)

            with dve.Fori(0, SEQS) as s:
                links = [0]

                def wait_for(ins):
                    links[0] += 1
                    ins.then_inc(att_chain, 1)
                    dve.wait_ge(att_chain, s * LINKS + links[0])

                def low(out, in_, high, bias_column=None):
                    if bias_column is None:
                        return dve.tensor_tensor(out, in_, high.bitcast(F32), ALU.subtract)
                    return dve.scalar_tensor_tensor(out=out, in0=in_, scalar=bias_column, in1=high.bitcast(F32),
                                                    op0=ALU.add, op1=ALU.subtract)

                def turned(t):
                    dve.wait_ge(turn_hi, s * T_FILLS + (t + 1))
                    return ps_turn[t % 2]

                def split(f):
                    dve.wait_ge(fill_hi, s * F_S + (f + 1))
                    return ps_share[f % 4]

                tiles = [x[:, bass.ds(s * ST + t, 1), :].rearrange("p a n -> p (a n)") for t in range(ST)]
                layer_norm(tiles, xs, wait_for, xs_ready)
                for tile in tiles:
                    dve.tensor_tensor(tile, tile, projb[:, :], ALU.add)
                for t in range(2):
                    low(xp_l[:, 2 * t:2 * t + 2, 1:SEQ + 1], turned(t)[:, :].rearrange("p (k n) -> p k n", k=2),
                        xp_h[:, 2 * t:2 * t + 2, 1:SEQ + 1]).then_inc(turn_lo, 1)
                for m in range(3):
                    src = split(m // 2)[:, m % 2 * SEQ:(m % 2 + 1) * SEQ]
                    ins = low(cT_l[:, m, :], src, cT_h[:, m, :], bias[:, B_CONV + m:B_CONV + m + 1])
                    if m:
                        ins.then_inc(fill_lo, 1)
                for f, hi, lo, col in ([(F_Q + n, qT_h, qT_l, B_Q) for n in range(4)]
                                       + [(F_K + n, kT_h, kT_l, B_K) for n in range(4)]):
                    src = split(f)
                    for e in range(2):
                        m = (f - F_Q) % 4 * 2 + e
                        ins = low(lo[:, m, :], src[:, e * SEQ:(e + 1) * SEQ], hi[:, m, :], bias[:, col + m:col + m + 1])
                    ins.then_inc(fill_lo, 1)
                for n in range(2 * ST):
                    part = slice(n % 2 * BANK, (n % 2 + 1) * BANK)
                    low(v_l[:, n // 2, part], split(F_V + n)[:, :], v_h[:, n // 2, part]).then_inc(fill_lo, 1)

                def maxima(u):
                    for e in range(2):
                        f = F_S + 2 * u + e
                        dve.wait_ge(fill_done, s * FILLS + (f + 1))
                        ins = dve.tensor_reduce(row_max[:, u % 2, 4 * e:4 * e + 4],
                                                ps_share[f % 4][:, :].rearrange("p (k n) -> p k n", k=4),
                                                AX_X, ALU.max)
                    wait_for(ins)
                    dve.tensor_scalar(neg_max[:, u % 2, :], row_max[:, u % 2, :], -SCALE, None,
                                      ALU.mult).then_inc(max_ready, 1)

                def probs_low(u):
                    for e in range(2):
                        low(pT_l[:, e, :], turned(2 + turn_of(u, e))[:, :], pT_h[:, e, :]).then_inc(turn_lo, 1)

                def heads_low(u):
                    low(hT_l[:, :, :].rearrange("p a n -> p (a n)"), turned(2 + turn_of(u, 2))[:, :],
                        hT_h[:, :, :].rearrange("p a n -> p (a n)")).then_inc(turn_lo, 1)

                def normalise(u):
                    dve.wait_ge(exp_done, s * 2 * UNITS + (2 * u + 2))
                    wait_for(dve.reciprocal(inv_sum[:, u % 2, :], row_sum[:, u % 2, :]))
                    dve.wait_ge(pv_done, s * UNITS + (u + 1))
                    dve.tensor_tensor(heads[:, u % 2, :].rearrange("p (h n) -> p h n", h=GH),
                                      ps_heads[:, :].rearrange("p (h n) -> p h n", h=GH),
                                      inv_sum[:, u % 2, :].unsqueeze(2).broadcast_to([P, GH, DH]),
                                      ALU.mult).then_inc(heads_ready, 1)

                maxima(0)
                for u in range(UNITS):
                    if u + 1 < UNITS:
                        maxima(u + 1)
                    probs_low(u)
                    if u:
                        heads_low(u - 1)
                    normalise(u)
                heads_low(UNITS - 1)
                dve.wait_ge(y_hi, s + 1)
                low(yT_l[:, :], ps_y[:, 0:SEQ], yT_h[:, :], out_bias[:, :]).then_inc(y_lo, 1)
                for b in range(ST):
                    dve.wait_ge(fill_done, s * FILLS + (F_OUT + b + 1))
                    dve.tensor_tensor(tiles[b], ps_share[(F_OUT + b) % 4][:, :], tiles[b],
                                      ALU.add).then_inc(x_attended, 1)
                assert links[0] == LINKS

            layer_norm([x[:, t, :] for t in range(HT)], xn[0], link, xn_ready)
            xT_low(2)
            w13_low(0, 2 * NT, 0, False)
            w2_low(0, 2 * NT, 0)
            layer_norm([x[:, HT + t, :] for t in range(HT)], xn[1], link, xn_ready)
            passes(2, True)
            passes(3, False)

        @block.tensor
        def _(pe):
            def product3(out, lhs, rhs, start, stop):
                pe.matmul(out, lhs[0], rhs[0], start=start, stop=False)
                pe.matmul(out, lhs[0], rhs[1], start=False, stop=False)
                return pe.matmul(out, lhs[1], rhs[0], start=False, stop=stop)

            def transpose_x(p):
                pe.wait_ge(xn_ready, p + 1)
                if p % 2:
                    pe.wait_ge(silu_done, NT * p)
                    pe.wait_ge(hid_ready, NT * p)
                for k in range(KT):
                    for t in range(HT):
                        last = pe.transpose(ps_xT[k][:, t * P:(t + 1) * P], xn[p % 2][:, t, k * P:(k + 1) * P],
                                            ident[:, :])
                    last.then_inc(xT_done, 1)

            def width_product(out, b, m):
                for k in range(KT):
                    last = product3(out, [w[:, b, m, k * P:(k + 1) * P] for w in (w13_h, w13_l)],
                                    [v[:, k, :] for v in (xT_h, xT_l)], k == 0, k == KT - 1)
                return last

            def gate0(t, b):
                pe.wait_ge(w13_lo, t + 1)
                at_least(pe, silu_done, t - 1)
                width_product(ps_gate[b][:, :], b, 0).then_inc(gate_done, 1)

            def gate_up(i, base, b, first):
                pe.wait_ge(w13_lo, i + (base + NT + 1))
                if not first:
                    at_least(pe, silu_done, i + (base - 1))
                    width_product(ps_gate[b][:, :], b, 0).then_inc(gate_done, 1)
                at_least(pe, hid_ready, i + (base - 1))
                width_product(ps_up[b][:, :], b, 1).then_inc(up_done, 1)

            def down(i, base, b, start, stop):
                pe.wait_ge(w2_lo, i + (base + 1))
                pe.wait_ge(hid_lo, i + (base + 1))
                if start:
                    at_least(pe, x_updated, HT * (base // NT))
                for t in range(HT):
                    last = product3(acc[t][:, :], [h[:, b, t * P:(t + 1) * P] for h in (hid_h, hid_l)],
                                    [w[:, b, :] for w in (w2_h, w2_l)], start, stop)
                last.then_inc(down_done, 1)

            def passes(p, carry_on):
                base, first = NT * p, p == 0
                pe.wait_ge(xT_lo, KT * (p + 1))
                gate_up(0, base, 0, first)
                gate_up(1, base, 1, first)
                down(0, base, 0, True, False)
                with pe.Fori(1, NT // 2) as j:
                    gate_up(j * 2, base, 0, first)
                    down(j * 2 - 1, base, 1, False, False)
                    gate_up(j * 2 + 1, base, 1, first)
                    down(j * 2, base, 0, False, False)
                if carry_on:
                    transpose_x(p + 1)
                down(NT - 1, base, 1, False, True)

            pe.wait_ge(const_ready, 3)
            transpose_x(0)
            pe.wait_ge(tot_ready, 1)
            pe.wait_ge(xT_lo, KT)
            pe.matmul(ps_up[0][:, 0:1], ones[:, :], abs_tot[:, 0:1], start=True, stop=True).then_inc(tot_sum, 1)
            gate0(0, 0)
            gate0(1, 1)
            with pe.Fori(1, NT // 2) as j:
                gate0(j * 2, 0)
                gate0(j * 2 + 1, 1)
            pe.wait_ge(tot_ready, 3)
            pe.matmul(ps_up[0][:, 1:3], ones[:, :], abs_tot[:, 1:3], start=True, stop=True).then_inc(tot_sum, 1)
            passes(0, True)
            passes(1, False)

            pe.wait_ge(small_loaded, 32)
            pe.wait_ge(x_updated, 2 * HT)
            for m in range(MT):
                c = AW + HD // BANK + m // 4
                if m % 4 == 0:
                    pe.wait_ge(aw_loaded[c % 2], 16 * (c // 2 + 1))
                last = pe.matmul(ps_y[:, 0:1], aw_raw[:, c % 2, m % 4 * P:(m % 4 + 1) * P],
                                 bias[:, B_V + m:B_V + m + 1], start=m == 0, stop=m == MT - 1)
                if m % 4 == 3:
                    last.then_inc(bias_sum, 1)
            pe.wait_ge(consts_r, 2)
            pe.wait_ge(pads_ready, 1)
            pe.wait_ge(aw_lo, AW + BW)
            pe.wait_ge(bias_ready, 1)

            with pe.Fori(0, SEQS) as s:
                def turn(t):
                    if t >= 2:
                        pe.wait_ge(turn_lo, s * T_FILLS + (t - 1))
                    return ps_turn[t % 2]

                def fill(f):
                    if f >= F_S + 4:
                        pe.wait_ge(exp_done, s * 2 * UNITS + (f - 4 - F_S + 1))
                    elif f >= 4:
                        pe.wait_ge(fill_lo, s * F_S + (f - 3))
                    return ps_share[f % 4]

                pe.wait_ge(xs_ready, s + 1)
                for t in range(2):
                    dst = turn(t)
                    for k in range(2):
                        for b in range(ST):
                            last = pe.transpose(dst[:, (k * ST + b) * P:(k * ST + b + 1) * P],
                                                xs[:, b, (2 * t + k) * P:(2 * t + k + 1) * P], ident[:, :])
                    last.then_inc(turn_done, 1)
                for m in range(3):
                    dst = fill(m // 2)[:, m % 2 * SEQ:(m % 2 + 1) * SEQ]
                    for k in range(KT):
                        if m == 0:
                            pe.wait_ge(turn_lo, s * T_FILLS + (k // 2 + 1))
                        for tap in range(TAPS):
                            last = product3(dst, [conv_w(w, tap, k, m) for w in (aw_h, aw_l)],
                                            [v[:, k, tap:tap + SEQ] for v in (xp_h, xp_l)],
                                            k == 0 and tap == 0, k == KT - 1 and tap == TAPS - 1)
                    if m:
                        last.then_inc(fill_done, 1)
                pe.wait_ge(fill_lo, s * F_S + 1)
                for f, col, c in [(F_Q + n, Q_COL, 0) for n in range(4)] + [(F_K + n, K_COL, 1) for n in range(4)]:
                    dst = fill(f)
                    for e in range(2):
                        m = (f - F_Q) % 4 * 2 + e
                        last = product3(dst[:, e * SEQ:(e + 1) * SEQ], [columns(w, col + m * P, P) for w in (aw_h, aw_l)],
                                        [v[:, c, :] for v in (cT_h, cT_l)], True, True)
                    last.then_inc(fill_done, 1)
                pe.wait_ge(fill_lo, s * F_S + 2)
                for n in range(2 * ST):
                    b = n // 2
                    product3(fill(F_V + n)[:, :], [v[:, 2, b * BLK:(b + 1) * BLK] for v in (cT_h, cT_l)],
                             [columns(w, V_COL + n % 2 * BANK, BANK) for w in (bw_h, bw_l)],
                             True, True).then_inc(fill_done, 1)

                def scores(u):
                    b, g = u // 2, u % 2
                    dst = [fill(F_S + 2 * u + e) for e in range(2)]
                    for e in range(2):
                        pe.matmul(dst[e][:, :], ident_r[:, :], mask_r[:, :, :].rearrange("p a n -> p (a n)"),
                                  start=True, stop=False)
                    for k in range(4):
                        for e in range(2):
                            rows = slice(e * DH, (e + 1) * DH)
                            last = product3(dst[e][:, k * BLK:(k + 1) * BLK],
                                            [v[rows, 4 * g + k, b * BLK:(b + 1) * BLK] for v in (qT_h, qT_l)],
                                            [v[rows, 4 * g + k, b * BLK:(b + 1) * BLK] for v in (kT_h, kT_l)],
                                            False, k == 3)
                            if k == 3:
                                last.then_inc(fill_done, 1)

                def turn_probs(u):
                    pe.wait_ge(exp_done, s * 2 * UNITS + (2 * u + 2))
                    for e in range(2):
                        dst = turn(2 + turn_of(u, e))
                        for k in range(4):
                            last = pe.transpose(dst[:, k * BLK:(k + 1) * BLK],
                                                probs[:, u % 2, e, k * BLK:(k + 1) * BLK], ident[:, :])
                        last.then_inc(turn_done, 1)

                def values(u):
                    b, g = u // 2, u % 2
                    pe.wait_ge(turn_lo, s * T_FILLS + (2 + turn_of(u, 1) + 1))
                    if u:
                        pe.wait_ge(heads_ready, s * UNITS + u)
                    for h in range(GH):
                        e, k = h % 2, h // 2
                        cols = slice((g * GH + h) * DH, (g * GH + h + 1) * DH)
                        last = product3(ps_heads[:, h * DH:(h + 1) * DH],
                                        [v[:, e, k * BLK:(k + 1) * BLK] for v in (pT_h, pT_l)],
                                        [v[:, b, cols] for v in (v_h, v_l)], True, True)
                    last.then_inc(pv_done, 1)

                def turn_heads(u):
                    pe.wait_ge(heads_ready, s * UNITS + (u + 1))
                    dst = turn(2 + turn_of(u, 2))
                    for m in range(4):
                        last = pe.transpose(dst[:, m * P:(m + 1) * P], heads[:, u % 2, m * P:(m + 1) * P], ident[:, :])
                    last.then_inc(turn_done, 1)

                def output(u):
                    b, g = u // 2, u % 2
                    pe.wait_ge(turn_lo, s * T_FILLS + (2 + turn_of(u, 2) + 1))
                    for m in range(4):
                        last = product3(ps_y[:, b * BLK:(b + 1) * BLK],
                                        [columns(w, O_COL + (4 * g + m) * W, W) for w in (bw_h, bw_l)],
                                        [v[:, m, :] for v in (hT_h, hT_l)], g == 0 and m == 0, g == 1 and m == 3)
                    last.then_inc(wo_done, 1)

                scores(0)
                for u in range(UNITS):
                    if u + 1 < UNITS:
                        scores(u + 1)
                    turn_probs(u)
                    if u:
                        turn_heads(u - 1)
                    values(u)
                    if u:
                        output(u - 1)
                turn_heads(UNITS - 1)
                output(UNITS - 1)
                pe.wait_ge(y_lo, s + 1)
                for b in range(ST):
                    product3(fill(F_OUT + b)[:, :], [v[:, b * BLK:(b + 1) * BLK] for v in (yT_h, yT_l)],
                             [columns(w, PROJ_COL, DM) for w in (bw_h, bw_l)], True, True).then_inc(fill_done, 1)

            transpose_x(2)
            passes(2, True)
            passes(3, False)


def kernel(**inputs):
    import numpy as _np
    import concourse.bacc as _bacc
    from concourse.bass_utils import run_bass_kernel_spmd as _run

    a = {n[3:]: _np.asarray(v) for n, v in inputs.items()}

    def inner_cols(w):
        return w.reshape(NT, P, KT, P).transpose(3, 0, 2, 1).reshape(P, NT, DM)

    def inner_rows(w):
        return w.reshape(DM, NT, P).transpose(2, 1, 0)

    def pair(w3, w2):
        return _np.stack([inner_cols(w3), inner_rows(w2)], axis=2).reshape(P, NT * 2 * DM)

    def columns(v):
        return v.reshape(-1, P).T

    attw = [a["attn_conv_w"].reshape(TAPS * KT, P, CONV_OUT).transpose(1, 0, 2), a["attn_wk"], a["attn_wq"],
            a["attn_wv"], a["attn_wo"].reshape(MT, P, W).transpose(1, 0, 2), a["attn_proj_w"]]
    biases = [columns(a["attn_" + n]) for n in ("conv_b", "bq", "bk", "bv", "bo")]
    arrays = {
        "x": a["attn_inputs"].reshape(TOK, DM),
        "w1": inner_cols(a["ffn_w1"]).reshape(P, NT * DM),
        "base1": inner_cols(a["ffn_mean_w1"]).reshape(P, NT * DM),
        "w23": pair(a["ffn_w3"], a["ffn_w2"]),
        "base23": pair(a["ffn_mean_w3"], a["ffn_mean_w2"]),
        "attw": _np.concatenate([v.reshape(P, -1) for v in attw], axis=1),
        "bias": _np.concatenate(biases, axis=1),
        "projb": a["attn_proj_b"],
    }
    arrays = {n: _np.ascontiguousarray(v) for n, v in arrays.items()}
    nc = _bacc.Bacc("TRN2", target_bir_lowering=False, num_devices=1, dynamic_dma_scratch_size=512)
    args = [nc.dram_tensor(n, v.shape, F32, kind="ExternalInput").ap() for n, v in arrays.items()]
    scratch = nc.dram_tensor("formed_weights", (P, NT * 3 * DM), F32, kind="Internal").ap()
    out = nc.dram_tensor("out", (TOK, DM), F32, kind="ExternalOutput").ap()
    macaron(nc, *args, scratch, out)
    r = _run(nc, [arrays], core_ids=[0])
    return r.results[0]["out"].reshape(SEQS, SEQ, DM)
```

```python
from contextlib import ExitStack

import concourse.bass as bass
from concourse import mybir

F32 = mybir.dt.float32
F32R = mybir.dt.float32r
I32 = mybir.dt.int32
I8 = mybir.dt.int8
ALU = mybir.AluOpType
ACT = mybir.ActivationFunctionType
AX_X = mybir.AxisListType.X

P = 128
BANK = 512
TOK = 1024
DM = 512
INTER = 1792
SEQS = 4
SEQ = TOK // SEQS
HALF = 512
KT = DM // P
NT = INTER // P
HT = HALF // P
W = 128
HEADS = 16
DH = 64
HD = HEADS * DH
BLK = 128
TAPS = 3
NEG = -1e30
EPS = 1e-5
RSQRT_MAGIC = float(0x5F3759DF)
RING = 4
CH1 = NT // 2
PREFETCH = 4
SCALE = DH ** -0.5
CONV_OUT = 3 * W
AW = TAPS * KT * CONV_OUT // BANK + 2 * HD // BANK
ST = SEQ // P
MT = HD // P
GH = 8
UNITS = ST * HEADS // GH
B_CONV, B_Q, B_K, B_V, B_O = 0, 3, 3 + MT, 3 + 2 * MT, 3 + 3 * MT
F_X, F_C, F_Q, F_K, F_V, FRONT = 0, 2, 5, 9, 13, 14


def at_least(eng, sem, value):
    if not (isinstance(value, int) and value <= 0):
        eng.wait_ge(sem, value)


def macaron(nc, x_in, w1_in, base1_in, w23_in, base23_in, attw_in, bias_in, projb_in, scratch, out):
    with ExitStack() as ctx:
        def at(name, shape, offset, dt=F32):
            return nc.alloc_sbuf_tensor_at(name, [P] + shape, dt, offset=offset)

        def sem(name):
            return ctx.enter_context(nc.semaphore(name))

        COMMON = 640
        x = at("x", [TOK // P, DM], COMMON)
        o = COMMON + 4 * TOK // P * DM
        ident = at("ident", [P], o)
        ones = at("ones", [P], o + 512)
        stats = at("stats", [HT, 6], o + 1024)
        newton = at("newton", [HT], o + 1120)
        varep = at("varep", [HT], o + 1152)
        mv = at("mv", [2 * HT, 2], o + 1184)
        rstd = at("rstd", [2 * HT], o + 1504)
        abs_sum = at("abs_sum", [3, NT], o + 1248)
        abs_tot = at("abs_tot", [3], o + 1440)
        coeff = at("coeff", [3], o + 1472)
        ident_r = at("ident_r", [P], o + 1536, F32R)
        mask_r = at("mask_r", [4, BLK], o + 2048, F32R)
        projb = at("projb", [DM], o + 4096)
        bias = at("bias", [B_O + 1], o + 6144)
        o = COMMON + 22656
        w13_h = at("w13_h", [2, 2, 512], o, F32R)
        w13_l = at("w13_l", [2, 2, 512], o + 8192, F32R)
        w2_h = at("w2_h", [2, DM], o + 16384, F32R)
        w2_l = at("w2_l", [2, DM], o + 20480, F32R)
        hid = at("hid", [2, HALF], o + 24576)
        hid_h = at("hid_h", [2, HALF], o + 28672, F32R)
        hid_l = at("hid_l", [2, HALF], o + 32768, F32R)
        xT_h = at("xT_h", [KT, HALF], o + 36864, F32R)
        xT_l = at("xT_l", [KT, HALF], o + 45056, F32R)
        WTS = o + 53248
        wts = at("wts", [NT, 3, 512], WTS)
        R3 = WTS + 4 * NT * 3 * 512
        sgn = at("sgn", [3, NT, 512], R3, I8)
        gates = at("gates", [NT, HALF], R3 + 21504)
        raw = at("raw", [RING, 1024], R3 + 50176)
        xn = [at("xn_a", [HT, DM], R3 + 21504), at("xn_b", [HT, DM], R3 + 57344)]

        mask_f = at("mask_f", [4, BLK], R3 + 21504 + 4 * 512 * (NT - 1))

        aw_h = at("aw_h", [AW, BANK], R3, F32R)
        aw_l = at("aw_l", [AW, BANK], R3 + 26624, F32R)
        aw_raw = at("aw_raw", [2, BANK], R3 + 53248)
        a = COMMON + 22656
        probs = at("probs", [2, GH * BLK], a)
        pT_h = at("pT_h", [2, 4 * BLK], a + 8192, F32R)
        pT_l = at("pT_l", [2, 4 * BLK], a + 12288, F32R)
        pw_h = at("pw_h", [DM], a + 16384, F32R)
        pw_l = at("pw_l", [DM], a + 18432, F32R)
        qT_h = at("qT_h", [MT, SEQ], a + 20480, F32R)
        qT_l = at("qT_l", [MT, SEQ], a + 28672, F32R)
        kT_h = at("kT_h", [MT, SEQ], a + 36864, F32R)
        kT_l = at("kT_l", [MT, SEQ], a + 45056, F32R)
        a = WTS + PREFETCH * 6144
        xp_h = at("xp_h", [KT, SEQ + 2], a, F32R)
        xp_l = at("xp_l", [KT, SEQ + 2], a + 4128, F32R)
        cT_h = at("cT_h", [2, SEQ], a + 8256, F32R)
        cT_l = at("cT_l", [2, SEQ], a + 10304, F32R)
        cv = at("cv", [SEQ], a + 12352)
        vt_h = at("vt_h", [ST, W], a + 13376, F32R)
        vt_l = at("vt_l", [ST, W], a + 14400, F32R)
        m_h = at("m_h", [HEADS, W], a + 15424, F32R)
        m_l = at("m_l", [HEADS, W], a + 23616, F32R)
        yT_h = at("yT_h", [SEQ], a + 31808, F32R)
        yT_l = at("yT_l", [SEQ], a + 32832, F32R)
        zT_h = at("zT_h", [2, 4, ST, BLK], a + 33856, F32R)
        zT_l = at("zT_l", [2, 4, ST, BLK], a + 42048, F32R)
        row_max = at("row_max", [2, GH], a + 50240)
        neg_max = at("neg_max", [2, GH], a + 50304)
        row_sum = at("row_sum", [2, GH], a + 50368)
        inv_sum = at("inv_sum", [2, GH], a + 50432)
        out_bias = at("out_bias", [1], a + 50496)
        mraw = [at("mraw_0", [2, BANK], R3 + 61440), at("mraw_1", [2, BANK], a + 50560)]
        xs = at("xs", [ST, DM], R3 + 57344)

        def columns(part, first, n):
            return part[:, :, :].rearrange("p c n -> p (c n)")[:, first:first + n]

        def conv_w(part, tap, k, m):
            return columns(part, (tap * KT + k) * CONV_OUT + m * W, W)

        K_COL = TAPS * KT * CONV_OUT
        Q_COL = K_COL + HD

        bank = [ctx.enter_context(nc.psum_tensor(f"bank{i}", [P, BANK], F32)) for i in range(8)]
        ps_gate, ps_up, acc = bank[0:2], bank[2:4], bank[4:8]
        ps_xT = bank[0:4]
        ps_front, ps_y, ps_turn, ps_score = bank[0:3], bank[3], bank[4:6], bank[6:8]
        ps_m = [bank[2], bank[3], bank[2], bank[3]]

        x_loaded = [sem("x_loaded_a"), sem("x_loaded_b")]
        raw_loaded = [sem(f"raw_loaded{i}") for i in range(RING)]
        diff_done = sem("diff_done")
        sign_done = sem("sign_done")
        abs_done = sem("abs_done")
        tot_ready = sem("tot_ready")
        tot_sum = sem("tot_sum")
        const_ready = sem("const_ready")
        dve_chain = sem("dve_chain")
        xn_ready = sem("xn_ready")
        xT_done = sem("xT_done")
        xT_hi = sem("xT_hi")
        xT_lo = sem("xT_lo")
        w1_formed = sem("w1_formed")
        w3_formed = sem("w3_formed")
        w2_formed = sem("w2_formed")
        w13_hi = sem("w13_hi")
        w13_lo = sem("w13_lo")
        w2_hi = sem("w2_hi")
        w2_lo = sem("w2_lo")
        gate_done = sem("gate_done")
        up_done = sem("up_done")
        down_done = sem("down_done")
        silu_done = sem("silu_done")
        hid_ready = sem("hid_ready")
        hid_hi = sem("hid_hi")
        hid_lo = sem("hid_lo")
        x_updated = sem("x_updated")
        w_saved = sem("w_saved")
        w_loaded = [sem("w_loaded_even"), sem("w_loaded_odd")]
        stored = sem("stored")
        small_loaded = sem("small_loaded")
        mask_ready = sem("mask_ready")
        consts_r = sem("consts_r")
        aw_loaded = [sem("aw_loaded_even"), sem("aw_loaded_odd")]
        aw_hi = sem("aw_hi")
        aw_lo = sem("aw_lo")
        mraw_loaded = [sem("mraw_loaded_0"), sem("mraw_loaded_1")]
        m_done = sem("m_done")
        m_hi = sem("m_hi")
        m_lo = sem("m_lo")
        bias_sum = sem("bias_sum")
        bias_ready = sem("bias_ready")
        xs_ready = sem("xs_ready")
        x_biased = sem("x_biased")
        front_done = sem("front_done")
        front_hi = sem("front_hi")
        front_lo = sem("front_lo")
        score_done = sem("score_done")
        max_found = sem("max_found")
        max_ready = sem("max_ready")
        exp_done = sem("exp_done")
        sum_inverted = sem("sum_inverted")
        norm_done = sem("norm_done")
        turn_done = sem("turn_done")
        turn_hi = sem("turn_hi")
        turn_lo = sem("turn_lo")
        z_done = sem("z_done")
        z_hi = sem("z_hi")
        z_lo = sem("z_lo")
        y_done = sem("y_done")
        y_hi = sem("y_hi")
        y_lo = sem("y_lo")
        out_done = sem("out_done")
        x_attended = sem("x_attended")

        def chunk_slot(k):
            return k % RING, k // RING + 1

        def split_of(f):
            return f + 1 if f < F_C + 2 else f

        block = ctx.enter_context(nc.Block())

        @block.sync
        def _(sp):
            def load_chunk1(k):
                at_least(sp, abs_done, k - RING + 1)
                at_least(sp, sign_done, k - RING + 1)
                slot, _ = chunk_slot(k)
                sp.dma_start(raw[:, slot, :], w1_in[:, 1024 * k:1024 * (k + 1)]).then_inc(raw_loaded[slot], 16)
                sp.dma_start(wts[:, 2 * k:2 * k + 2, 0, :],
                             base1_in[:, 1024 * k:1024 * (k + 1)].rearrange("p (t n) -> p t n", t=2)
                             ).then_inc(raw_loaded[slot], 16)

            def load_chunk23(t, slot):
                at_least(sp, abs_done, t + (CH1 - RING + 1))
                at_least(sp, sign_done, t + (CH1 - RING + 1))
                sp.dma_start(raw[:, slot, :], w23_in[:, bass.ds(t * 1024, 1024)]).then_inc(raw_loaded[slot], 16)
                sp.dma_start(wts[:, bass.ds(t, 1), 1:3, :].rearrange("p a b n -> p (a b) n"),
                             base23_in[:, bass.ds(t * 1024, 1024)].rearrange("p (t n) -> p t n", t=2)
                             ).then_inc(raw_loaded[slot], 16)

            def load_attw_chunk(c, slot):
                at_least(sp, aw_hi, c - 1)
                at_least(sp, aw_lo, c - 1)
                sp.dma_start(aw_raw[:, slot, :], attw_in[:, bass.ds(c * BANK, BANK)]).then_inc(aw_loaded[slot], 16)

            def load_attw(c0, c1, first):
                if first:
                    sp.wait_ge(abs_done, CH1 + NT)
                    sp.wait_ge(sign_done, CH1 + NT)
                for c in range(c0, c0 + 2):
                    load_attw_chunk(c, c % 2)
                with sp.Fori(1, (c1 - c0) // 2) as j:
                    for q in range(2):
                        load_attw_chunk(j * 2 + (c0 + q), (c0 + q) % 2)
                if (c1 - c0) % 2:
                    load_attw_chunk(c1 - 1, (c1 - 1) % 2)

            def load_formed(i, slot, j):
                at_least(sp, w_loaded[slot], j * 16)
                sp.dma_start(wts[:, bass.ds(i, 1), :, :].rearrange("p a b n -> p (a b n)"),
                             scratch[:, bass.ds(i * 1536, 1536)]).then_inc(w_loaded[slot], 16)

            for k in range(2):
                load_chunk1(k)
            xv = x_in.rearrange("(t p) d -> p t d", p=P)
            sp.dma_start(x[:, 0:HT, :], xv[:, 0:HT, :]).then_inc(x_loaded[0], 16)
            sp.dma_start(bias[:, :], bias_in).then_inc(small_loaded, 16)
            sp.dma_start(projb[:, :], projb_in.partition_broadcast(P)).then_inc(small_loaded, 16)
            for k in range(2, CH1):
                load_chunk1(k)
            for t in range(2):
                load_chunk23(t, chunk_slot(CH1 + t)[0])
            with sp.Fori(0, (NT - 2) // 4) as j:
                for q in range(4):
                    load_chunk23(j * 4 + (2 + q), chunk_slot(CH1 + 2 + q)[0])
            sp.dma_start(x[:, HT:2 * HT, :], xv[:, HT:2 * HT, :]).then_inc(x_loaded[1], 16)
            with sp.Fori(0, NT) as i:
                sp.wait_ge(w2_formed, i + 1)
                sp.dma_start(scratch[:, bass.ds(i * 1536, 1536)],
                             wts[:, bass.ds(i, 1), :, :].rearrange("p a b n -> p (a b n)")).then_inc(w_saved, 16)
            load_attw(0, AW + 1, True)
            for g in range(2):
                if g:
                    sp.wait_ge(w_saved, 16 * NT)
                    sp.wait_ge(w2_lo, 2 * NT)
                sp.dma_start(mraw[g][:, :, :].rearrange("p a n -> p (a n)"),
                             attw_in[:, (AW + 1 + 2 * g) * BANK:(AW + 3 + 2 * g) * BANK]).then_inc(mraw_loaded[g], 16)
            for i in range(PREFETCH):
                load_formed(i, i % 2, i // 2)
            sp.wait_ge(x_attended, 2 * HT)
            with sp.Fori(PREFETCH // 2, NT // 2) as j:
                for q in range(2):
                    load_formed(j * 2 + q, q, j)
            for t in range(2 * HT):
                sp.wait_ge(x_updated, 2 * HT + t + 1)
                sp.dma_start(out[t * P:(t + 1) * P, :], x[:, t, :]).then_inc(stored, 16)
            sp.wait_ge(stored, 16 * 2 * HT)

        @block.gpsimd
        def _(pool):
            pool.memset(ident[:, :], 0.0).then_inc(const_ready, 1)
            pool.memset(ones[:, :], 1.0).then_inc(const_ready, 1)
            pool.wait_ge(const_ready, 2)
            pool.affine_select(out=ident[:, :], in_=ident[:, :], compare_op=ALU.not_equal, fill=1.0,
                               base=0, pattern=[[-1, P]], channel_multiplier=1).then_inc(const_ready, 1)
            pool.memset(mask_f[:, :, :], 0.0).then_inc(mask_ready, 1)
            pool.wait_ge(mask_ready, 1)
            pool.affine_select(out=mask_f[:, :, :], in_=mask_f[:, :, :], compare_op=ALU.is_ge, fill=NEG,
                               base=0, pattern=[[0, 4], [-1, BLK]], channel_multiplier=1).then_inc(mask_ready, 1)

            def diff1(k):
                slot, use = chunk_slot(k)
                pool.wait_ge(raw_loaded[slot], 32 * use)
                r = raw[:, slot, :].rearrange("p (t n) -> p t n", t=2)
                pool.tensor_tensor(r, r, wts[:, 2 * k:2 * k + 2, 0, :], ALU.subtract).then_inc(diff_done, 1)

            def diff23(t, slot, use):
                pool.wait_ge(raw_loaded[slot], use * 32)
                pool.tensor_tensor(raw[:, slot, :], raw[:, slot, :],
                                   wts[:, bass.ds(t, 1), 1:3, :].rearrange("p a b n -> p (a b n)"),
                                   ALU.subtract).then_inc(diff_done, 1)

            for k in range(CH1):
                diff1(k)
            for t in range(2):
                diff23(t, *chunk_slot(CH1 + t))
            with pool.Fori(0, (NT - 2) // 4) as j:
                for q in range(4):
                    slot, use = chunk_slot(CH1 + 2 + q)
                    diff23(j * 4 + (2 + q), slot, j + use)

            pool.wait_ge(small_loaded, 32)
            with pool.Fori(0, SEQS) as s:
                pool.wait_ge(xs_ready, s + 1)
                for t in range(ST):
                    tile = x[:, bass.ds(s * ST + t, 1), :].rearrange("p a n -> p (a n)")
                    pool.tensor_tensor(tile, tile, projb[:, :], ALU.add).then_inc(x_biased, 1)

        @block.scalar
        def _(act):
            def sign1(k):
                act.wait_ge(diff_done, k + 1)
                slot, _ = chunk_slot(k)
                act.activation(sgn[:, 0, 2 * k:2 * k + 2, :],
                               raw[:, slot, :].rearrange("p (t n) -> p t n", t=2), ACT.Sign).then_inc(sign_done, 1)

            def sign23(t, slot):
                act.wait_ge(diff_done, t + (CH1 + 1))
                act.activation(sgn[:, 1:3, bass.ds(t, 1), :].rearrange("p a b n -> p a (b n)"),
                               raw[:, slot, :].rearrange("p (t n) -> p t n", t=2), ACT.Sign).then_inc(sign_done, 1)

            def xT_high(p):
                for k in range(KT):
                    act.wait_ge(xT_done, KT * p + k + 1)
                    act.activation(xT_h[:, k, :], ps_xT[k][:, :], ACT.Copy).then_inc(xT_hi, 1)

            def w1_high(t, b):
                act.wait_ge(w1_formed, t + 1)
                at_least(act, gate_done, t - 1)
                act.activation(w13_h[:, b, 0, :], wts[:, bass.ds(t, 1), 0, :].rearrange("p a n -> p (a n)"),
                               ACT.Copy).then_inc(w13_hi, 1)

            def silu_store(t, b):
                act.wait_ge(gate_done, t + 1)
                act.activation(gates[:, bass.ds(t, 1), :].rearrange("p a n -> p (a n)"), ps_gate[b][:, :],
                               ACT.Silu).then_inc(silu_done, 1)

            def w13_high(i, base, b, first):
                if first:
                    act.wait_ge(w3_formed, i + 1)
                at_least(act, up_done, i + (base - 1))
                src = wts[:, bass.ds(i, 1), 1 if first else 0:2, :].rearrange("p a b n -> p (a b) n")
                act.activation(w13_h[:, b, 1 if first else 0:2, :], src, ACT.Copy).then_inc(w13_hi, 1)

            def w2_high(i, base, b, first):
                if first:
                    act.wait_ge(w2_formed, i + 1)
                at_least(act, down_done, i + (base - 1))
                act.activation(w2_h[:, b, :], wts[:, bass.ds(i, 1), 2, :].rearrange("p a n -> p (a n)"),
                               ACT.Copy).then_inc(w2_hi, 1)

            def hid_high(i, base, b, first):
                act.wait_ge(hid_ready, i + (base + 1))
                at_least(act, down_done, i + (base - 1))
                src = gates[:, bass.ds(i, 1), :].rearrange("p a n -> p (a n)") if first else hid[:, b, :]
                act.activation(hid_h[:, b, :], src, ACT.Copy).then_inc(hid_hi, 1)

            def silu(i, base, b):
                act.wait_ge(gate_done, i + (base + 1))
                at_least(act, hid_lo, i + (base - 1))
                act.activation(hid[:, b, :], ps_gate[b][:, :], ACT.Silu).then_inc(silu_done, 1)

            def attw_high(c, slot, use):
                act.wait_ge(aw_loaded[slot], use * 16)
                act.activation(aw_h[:, bass.ds(c, 1), :].rearrange("p a n -> p (a n)"), aw_raw[:, slot, :],
                               ACT.Copy).then_inc(aw_hi, 1)

            def step(i, base, b, first, pair):
                if base == 2 * NT:
                    act.wait_ge(w_loaded[b], pair * 16 + 16)
                if base == NT:
                    attw_high(i - 1, 1 - b, pair + b)
                w13_high(i, base, b, first)
                if not first:
                    silu(i - 1, base, 1 - b)
                hid_high(i - 1, base, 1 - b, first)
                w2_high(i, base, b, first)

            def passes(p, carry_on):
                base, first = NT * p, p == 0
                step(1, base, 1, first, 0)
                with act.Fori(1, NT // 2) as j:
                    step(j * 2, base, 0, first, j)
                    step(j * 2 + 1, base, 1, first, j)
                if carry_on:
                    w13_high(0, base + NT, 0, False)
                if not first:
                    silu(NT - 1, base, 1)
                hid_high(NT - 1, base, 1, first)
                if carry_on:
                    w2_high(0, base + NT, 0, False)
                    xT_high(p + 1)

            act.wait_ge(const_ready, 3)
            act.activation(ident_r[:, :], ident[:, :], ACT.Copy).then_inc(consts_r, 1)
            act.wait_ge(mask_ready, 2)
            act.activation(mask_r[:, :, :], mask_f[:, :, :], ACT.Copy).then_inc(consts_r, 1)
            for k in range(CH1):
                sign1(k)
            xT_high(0)
            w1_high(0, 0)
            w1_high(1, 1)
            silu_store(0, 0)
            sign23(0, chunk_slot(CH1)[0])
            with act.Fori(0, (NT - 2) // 4) as j:
                for q in range(4):
                    t = j * 4 + (2 + q)
                    w1_high(t, q % 2)
                    silu_store(t - 1, 1 - q % 2)
                    sign23(t - 1, chunk_slot(CH1 + 1 + q)[0])
            silu_store(NT - 1, 1)
            sign23(NT - 1, chunk_slot(CH1 + NT - 1)[0])
            w13_high(0, 0, 0, True)
            w2_high(0, 0, 0, True)
            passes(0, True)
            act.wait_ge(hid_lo, NT)
            passes(1, False)

            def high(out, in_, bias_column=None):
                if bias_column is None:
                    return act.activation(out, in_, ACT.Copy)
                return act.activation(out, in_, ACT.Identity, bias=bias_column)

            def front(n, f):
                act.wait_ge(front_done, n * FRONT + (f + 1))
                src = ps_front[f % 3]
                if f < F_C:
                    ins = high(xp_h[:, 2 * f:2 * f + 2, 1:SEQ + 1], src[:, :].rearrange("p (k n) -> p k n", k=2))
                elif f < F_Q:
                    m = f - F_C
                    ins = high(cT_h[:, m, :], src[:, 0:SEQ], bias[:, B_CONV + m:B_CONV + m + 1])
                elif f < F_V:
                    part, col = (qT_h, B_Q) if f < F_K else (kT_h, B_K)
                    for e in range(2):
                        m = (f - F_Q) % 4 * 2 + e
                        ins = high(part[:, m, :], src[:, e * SEQ:(e + 1) * SEQ], bias[:, col + m:col + m + 1])
                else:
                    ins = high(vt_h[:, :, :].rearrange("p b n -> p (b n)"), src[:, 0:SEQ])
                ins.then_inc(front_hi, 1)

            def exps(s, u):
                act.wait_ge(max_ready, s * UNITS + (u + 1))
                for e in range(2):
                    for k in range(4):
                        h = 4 * e + k
                        ins = act.activation(probs[:, u % 2, h * BLK:(h + 1) * BLK],
                                             ps_score[e][:, k * BLK:(k + 1) * BLK], ACT.Exp,
                                             bias=neg_max[:, u % 2, h:h + 1], scale=SCALE,
                                             accum_out=row_sum[:, u % 2, h:h + 1])
                    ins.then_inc(exp_done, 1)

            def probs_high(s, u):
                for e in range(2):
                    act.wait_ge(turn_done, s * 2 * UNITS + (2 * u + e + 1))
                    high(pT_h[:, e, :], ps_turn[e][:, :]).then_inc(turn_hi, 1)

            def z_high(s, u):
                for e in range(2):
                    act.wait_ge(z_done, s * 2 * UNITS + (2 * u + e + 1))
                    high(zT_h[:, e, :, u % ST, :], ps_turn[e][:, :].rearrange("p (k n) -> p k n", k=4)).then_inc(z_hi, 1)

            def y_high(s):
                act.wait_ge(y_done, s + 1)
                high(yT_h[:, :], ps_y[:, 0:SEQ], out_bias[:, :]).then_inc(y_hi, 1)

            def attend(s, n):
                def fronts(first, last):
                    if n is not None:
                        for f in range(first, last):
                            front(n, f)

                fronts(F_X, F_C)
                exps(s, 0)
                fronts(F_C, F_C + 1)
                probs_high(s, 0)
                exps(s, 1)
                fronts(F_C + 1, F_C + 2)
                z_high(s, 0)
                probs_high(s, 1)
                exps(s, 2)
                z_high(s, 1)
                fronts(F_Q, F_Q + 2)
                probs_high(s, 2)
                exps(s, 3)
                z_high(s, 2)
                fronts(F_Q + 2, F_K + 2)
                probs_high(s, 3)
                fronts(F_K + 2, F_K + 3)
                z_high(s, 3)
                fronts(F_K + 3, F_V)
                y_high(s)
                fronts(F_V, FRONT)

            act.wait_ge(w_saved, 16 * NT)
            act.wait_ge(w2_lo, 2 * NT)
            act.wait_ge(small_loaded, 32)
            for f in range(F_X, F_C):
                front(0, f)
            for q in range(4):
                act.wait_ge(m_done, q + 1)
                high(m_h[:, 4 * q:4 * q + 4, :].rearrange("p a n -> p (a n)"), ps_m[q][:, :]).then_inc(m_hi, 1)
            act.wait_ge(down_done, 2 * NT)
            act.wait_ge(aw_loaded[AW % 2], 16 * (AW // 2 + 1))
            high(pw_h[:, :], aw_raw[:, AW % 2, :]).then_inc(aw_hi, 1)
            for f in range(F_C, FRONT):
                if f != F_C + 2:
                    front(0, f)
            act.wait_ge(bias_ready, 1)
            with act.Fori(0, SEQS - 1) as s:
                attend(s, s + 1)
            attend(SEQS - 1, None)

            act.wait_ge(x_attended, 2 * HT)
            act.wait_ge(w_loaded[0], 16)
            xT_high(2)
            w13_high(0, 2 * NT, 0, False)
            w2_high(0, 2 * NT, 0, False)
            passes(2, True)
            passes(3, False)

        @block.vector
        def _(dve):
            chain = [0]

            def link(ins):
                chain[0] += 1
                ins.then_inc(dve_chain, 1)
                dve.wait_ge(dve_chain, chain[0])

            def norm_stats(p):
                half = slice(HT * p, HT * (p + 1))
                for t in range(HT):
                    last = dve.bn_stats(stats[:, t, :], x[:, HT * p + t, :])
                link(last)
                v, r, w = varep[:, :], rstd[:, half], newton[:, :]
                dve.memset(v, EPS)
                for t in range(HT):
                    last = dve.bn_aggr(mv[:, HT * p + t, :], stats[:, t, :])
                link(last)
                link(dve.tensor_tensor(v, mv[:, half, 1], v, ALU.add))
                link(dve.tensor_scalar(r.bitcast(I32), v.bitcast(I32), -0.5, RSQRT_MAGIC, ALU.mult, ALU.add))
                for _ in range(3):
                    link(dve.scalar_tensor_tensor(out=w, in0=r, scalar=-0.5, in1=r, op0=ALU.mult, op1=ALU.mult))
                    link(dve.tensor_tensor(w, w, v, ALU.mult))
                    link(dve.scalar_tensor_tensor(out=r, in0=w, scalar=1.5, in1=r, op0=ALU.add, op1=ALU.mult))

            def normalise(p):
                for t in range(HT * p, HT * (p + 1)):
                    last = dve.tensor_scalar(xn[p][:, t - HT * p, :], x[:, t, :], mv[:, t, 0:1], rstd[:, t:t + 1],
                                             ALU.subtract, ALU.mult)
                last.then_inc(xn_ready, 1)

            def xT_low(p):
                for k in range(KT):
                    dve.wait_ge(xT_hi, KT * p + k + 1)
                    dve.tensor_tensor(xT_l[:, k, :], ps_xT[k][:, :], xT_h[:, k, :].bitcast(F32),
                                      ALU.subtract).then_inc(xT_lo, 1)

            def sum_abs1(k):
                dve.wait_ge(diff_done, k + 1)
                dve.tensor_reduce(abs_sum[:, 0, k:k + 1], raw[:, chunk_slot(k)[0], :], AX_X, ALU.add,
                                  apply_absolute_value=True).then_inc(abs_done, 1)

            def sum_abs23(t, slot):
                dve.wait_ge(diff_done, t + (CH1 + 1))
                dve.tensor_reduce(abs_sum[:, 1:3, bass.ds(t, 1)].rearrange("p a b -> p (a b)"),
                                  raw[:, slot, :].rearrange("p (a n) -> p a n", a=2),
                                  AX_X, ALU.add, apply_absolute_value=True).then_inc(abs_done, 1)

            def form(m, i, done):
                place = wts[:, bass.ds(i, 1), m, :].rearrange("p a n -> p (a n)")
                dve.scalar_tensor_tensor(out=place, in0=sgn[:, m, bass.ds(i, 1), :].rearrange("p a n -> p (a n)"),
                                         scalar=coeff[:, m:m + 1], in1=place, op0=ALU.mult,
                                         op1=ALU.add).then_inc(done, 1)

            def w1_low(t, b):
                dve.wait_ge(w13_hi, t + 1)
                at_least(dve, gate_done, t - 1)
                dve.tensor_tensor(w13_l[:, b, 0, :], wts[:, bass.ds(t, 1), 0, :].rearrange("p a n -> p (a n)"),
                                  w13_h[:, b, 0, :].bitcast(F32), ALU.subtract).then_inc(w13_lo, 1)

            def w13_low(i, base, b, first):
                dve.wait_ge(w13_hi, i + (base + NT + 1))
                lo = 1 if first else 0
                src = wts[:, bass.ds(i, 1), lo:2, :].rearrange("p a b n -> p (a b) n")
                dve.tensor_tensor(w13_l[:, b, lo:2, :], src, w13_h[:, b, lo:2, :].bitcast(F32),
                                  ALU.subtract).then_inc(w13_lo, 1)

            def w2_low(i, base, b):
                dve.wait_ge(w2_hi, i + (base + 1))
                dve.tensor_tensor(w2_l[:, b, :], wts[:, bass.ds(i, 1), 2, :].rearrange("p a n -> p (a n)"),
                                  w2_h[:, b, :].bitcast(F32), ALU.subtract).then_inc(w2_lo, 1)

            def hidden(i, base, b, first):
                dve.wait_ge(silu_done, i + (base + 1))
                dve.wait_ge(up_done, i + (base + 1))
                h = gates[:, bass.ds(i, 1), :].rearrange("p a n -> p (a n)") if first else hid[:, b, :]
                dve.tensor_tensor(h, h, ps_up[b][:, :], ALU.mult).then_inc(hid_ready, 1)
                dve.wait_ge(hid_hi, i + (base + 1))
                dve.tensor_tensor(hid_l[:, b, :], h, hid_h[:, b, :].bitcast(F32), ALU.subtract).then_inc(hid_lo, 1)

            def attw_low(c, slot):
                dve.wait_ge(aw_hi, c + 1)
                high, low = (v[:, bass.ds(c, 1), :].rearrange("p a n -> p (a n)") for v in (aw_h, aw_l))
                dve.tensor_tensor(low, aw_raw[:, slot, :], high.bitcast(F32), ALU.subtract).then_inc(aw_lo, 1)

            def low(out, in_, high, bias_column=None):
                if bias_column is None:
                    return dve.tensor_tensor(out, in_, high.bitcast(F32), ALU.subtract)
                return dve.scalar_tensor_tensor(out=out, in0=in_, scalar=bias_column, in1=high.bitcast(F32),
                                                op0=ALU.add, op1=ALU.subtract)

            def sequence_norm(n):
                for t in range(ST):
                    i = bass.ds(n * ST + t, 1)
                    ins = dve.tensor_scalar(xs[:, t, :], x[:, i, :].rearrange("p a n -> p (a n)"),
                                            mv[:, i, 0:1].rearrange("p a n -> p (a n)"), rstd[:, i],
                                            ALU.subtract, ALU.mult)
                ins.then_inc(xs_ready, 1)

            def front(n, f):
                if f == F_C + 2:
                    dve.wait_ge(front_done, n * FRONT + (f + 1))
                else:
                    dve.wait_ge(front_hi, n * (FRONT - 1) + split_of(f))
                src = ps_front[f % 3]
                if f < F_C:
                    ins = low(xp_l[:, 2 * f:2 * f + 2, 1:SEQ + 1], src[:, :].rearrange("p (k n) -> p k n", k=2),
                              xp_h[:, 2 * f:2 * f + 2, 1:SEQ + 1])
                elif f < F_C + 2:
                    m = f - F_C
                    ins = low(cT_l[:, m, :], src[:, 0:SEQ], cT_h[:, m, :], bias[:, B_CONV + m:B_CONV + m + 1])
                elif f == F_C + 2:
                    ins = dve.tensor_scalar(cv[:, :], src[:, 0:SEQ], bias[:, B_CONV + 2:B_CONV + 3], None, ALU.add)
                elif f < F_V:
                    hi, lo, col = (qT_h, qT_l, B_Q) if f < F_K else (kT_h, kT_l, B_K)
                    for e in range(2):
                        m = (f - F_Q) % 4 * 2 + e
                        ins = low(lo[:, m, :], src[:, e * SEQ:(e + 1) * SEQ], hi[:, m, :], bias[:, col + m:col + m + 1])
                else:
                    ins = low(vt_l[:, :, :].rearrange("p b n -> p (b n)"), src[:, 0:SEQ],
                              vt_h[:, :, :].rearrange("p b n -> p (b n)"))
                ins.then_inc(front_lo, 1)

            def maxima(s, u):
                for e in range(2):
                    dve.wait_ge(score_done, s * 2 * UNITS + (2 * u + e + 1))
                    ins = dve.tensor_reduce(row_max[:, u % 2, 4 * e:4 * e + 4],
                                            ps_score[e][:, :].rearrange("p (k n) -> p k n", k=4), AX_X, ALU.max)
                ins.then_inc(max_found, 1)
                dve.wait_ge(max_found, s * UNITS + (u + 1))
                dve.tensor_scalar(neg_max[:, u % 2, :], row_max[:, u % 2, :], -SCALE, None,
                                  ALU.mult).then_inc(max_ready, 1)

            def probabilities(s, u):
                dve.wait_ge(exp_done, s * 2 * UNITS + (2 * u + 2))
                dve.reciprocal(inv_sum[:, u % 2, :], row_sum[:, u % 2, :]).then_inc(sum_inverted, 1)
                dve.wait_ge(sum_inverted, s * UNITS + (u + 1))
                p = probs[:, u % 2, :].rearrange("p (h n) -> p h n", h=GH)
                dve.tensor_tensor(p, p, inv_sum[:, u % 2, :].unsqueeze(2).broadcast_to([P, GH, BLK]),
                                  ALU.mult).then_inc(norm_done, 1)

            def probs_low(s, u):
                for e in range(2):
                    dve.wait_ge(turn_hi, s * 2 * UNITS + (2 * u + e + 1))
                    low(pT_l[:, e, :], ps_turn[e][:, :], pT_h[:, e, :]).then_inc(turn_lo, 1)

            def z_low(s, u):
                for e in range(2):
                    dve.wait_ge(z_hi, s * 2 * UNITS + (2 * u + e + 1))
                    low(zT_l[:, e, :, u % ST, :], ps_turn[e][:, :].rearrange("p (k n) -> p k n", k=4),
                        zT_h[:, e, :, u % ST, :]).then_inc(z_lo, 1)

            def y_low(s):
                dve.wait_ge(y_hi, s + 1)
                low(yT_l[:, :], ps_y[:, 0:SEQ], yT_h[:, :], out_bias[:, :]).then_inc(y_lo, 1)

            def output(s):
                dve.wait_ge(x_biased, s * ST + ST)
                for b in range(ST):
                    dve.wait_ge(out_done, s * ST + (b + 1))
                    tile = x[:, bass.ds(s * ST + b, 1), :].rearrange("p a n -> p (a n)")
                    dve.tensor_tensor(tile, ps_turn[b][:, :], tile, ALU.add).then_inc(x_attended, 1)

            def attend(s, n):
                def fronts(first, last):
                    if n is not None:
                        for f in range(first, last):
                            front(n, f)

                if n is not None:
                    sequence_norm(n)
                fronts(F_X, F_C)
                probabilities(s, 0)
                fronts(F_C, F_C + 1)
                maxima(s, 1)
                probs_low(s, 0)
                probabilities(s, 1)
                fronts(F_C + 1, F_C + 2)
                z_low(s, 0)
                maxima(s, 2)
                probs_low(s, 1)
                fronts(F_C + 2, F_Q)
                probabilities(s, 2)
                z_low(s, 1)
                fronts(F_Q, F_Q + 1)
                maxima(s, 3)
                fronts(F_Q + 1, F_Q + 2)
                probs_low(s, 2)
                probabilities(s, 3)
                z_low(s, 2)
                fronts(F_Q + 2, F_K + 2)
                probs_low(s, 3)
                fronts(F_K + 2, F_K + 3)
                if n is None:
                    dve.wait_ge(x_attended, HT)
                    norm_stats(0)
                    normalise(0)
                z_low(s, 3)
                fronts(F_K + 3, F_V)
                y_low(s)
                if n is not None:
                    maxima(n, 0)
                fronts(F_V, FRONT)
                output(s)

            def first_front():
                dve.wait_ge(w_saved, 16 * NT)
                for part in (xp_h, xp_l):
                    for column in (0, SEQ + 1):
                        dve.memset(part[:, :, column:column + 1].bitcast(F32), 0.0)
                for f in range(F_X, F_C):
                    front(0, f)
                for q in range(4):
                    dve.wait_ge(m_hi, q + 1)
                    high, low_part = (v[:, 4 * q:4 * q + 4, :].rearrange("p a n -> p (a n)") for v in (m_h, m_l))
                    low(low_part, ps_m[q][:, :], high).then_inc(m_lo, 1)

            def step(i, base, b, first):
                if base == NT:
                    attw_low(i - 1, 1 - b)
                if first:
                    form(1, i, w3_formed)
                    form(2, i, w2_formed)
                w13_low(i, base, b, first)
                hidden(i - 1, base, 1 - b, first)
                w2_low(i, base, b)

            def passes(p, carry_on):
                base, first = NT * p, p == 0
                step(1, base, 1, first)
                if p == 1:
                    dve.wait_ge(x_updated, HT)
                    norm_stats(0)
                    sequence_norm(0)
                with dve.Fori(1, NT // 2) as j:
                    step(j * 2, base, 0, first)
                    step(j * 2 + 1, base, 1, first)
                if carry_on:
                    w13_low(0, base + NT, 0, False)
                hidden(NT - 1, base, 1, first)
                if carry_on:
                    w2_low(0, base + NT, 0)
                    xT_low(p + 1)
                if p == 1:
                    first_front()
                dve.wait_ge(down_done, base + NT)
                for t in range(HT):
                    tile = x[:, HT * p % (2 * HT) + t, :]
                    dve.scalar_tensor_tensor(out=tile, in0=acc[t][:, :], scalar=0.5, in1=tile, op0=ALU.mult,
                                             op1=ALU.add).then_inc(x_updated, 1)

            def total(m, n):
                dve.tensor_reduce(abs_tot[:, m:m + 1], abs_sum[:, m, 0:n], AX_X, ALU.add).then_inc(tot_ready, 1)

            def mean(m, col):
                link(dve.tensor_scalar(coeff[:, m:m + 1], ps_up[0][:, col:col + 1], 1.0 / (INTER * DM), None, ALU.mult))

            for k in range(CH1):
                sum_abs1(k)
                if k == 2:
                    dve.wait_ge(x_loaded[0], 16)
                    norm_stats(0)
                    normalise(0)
            xT_low(0)
            dve.wait_ge(abs_done, CH1)
            total(0, CH1)
            dve.wait_ge(tot_sum, 1)
            dve.wait_ge(sign_done, CH1)
            mean(0, 0)
            form(0, 0, w1_formed)
            w1_low(0, 0)
            form(0, 1, w1_formed)
            w1_low(1, 1)
            sum_abs23(0, chunk_slot(CH1)[0])
            with dve.Fori(0, (NT - 2) // 4) as j:
                for q in range(4):
                    t = j * 4 + (2 + q)
                    form(0, t, w1_formed)
                    w1_low(t, q % 2)
                    sum_abs23(t - 1, chunk_slot(CH1 + 1 + q)[0])
            sum_abs23(NT - 1, chunk_slot(CH1 + NT - 1)[0])
            dve.wait_ge(abs_done, CH1 + NT)
            total(1, NT)
            total(2, NT)
            dve.wait_ge(x_loaded[1], 16)
            dve.wait_ge(tot_sum, 2)
            dve.wait_ge(sign_done, CH1 + NT)
            mean(1, 1)
            mean(2, 2)
            form(1, 0, w3_formed)
            form(2, 0, w2_formed)
            w13_low(0, 0, 0, True)
            w2_low(0, 0, 0)
            norm_stats(1)
            normalise(1)
            passes(0, True)
            passes(1, False)

            dve.wait_ge(aw_hi, AW + 1)
            low(pw_l[:, :], aw_raw[:, AW % 2, :], pw_h[:, :]).then_inc(aw_lo, 1)
            dve.wait_ge(small_loaded, 32)
            front(0, F_C)
            dve.wait_ge(x_updated, 2 * HT)
            norm_stats(1)
            front(0, F_C + 1)
            dve.wait_ge(bias_sum, 1)
            dve.tensor_tensor(out_bias[:, :], ps_turn[0][:, 0:1], bias[:, B_O:B_O + 1], ALU.add).then_inc(bias_ready, 1)
            for f in range(F_C + 2, FRONT):
                front(0, f)
            maxima(0, 0)
            with dve.Fori(0, SEQS - 1) as s:
                attend(s, s + 1)
            attend(SEQS - 1, None)

            xT_low(2)
            w13_low(0, 2 * NT, 0, False)
            w2_low(0, 2 * NT, 0)
            dve.wait_ge(x_attended, 2 * HT)
            norm_stats(1)
            normalise(1)
            passes(2, True)
            passes(3, False)

        @block.tensor
        def _(pe):
            def product3(out, lhs, rhs, start, stop):
                pe.matmul(out, lhs[0], rhs[0], start=start, stop=False)
                pe.matmul(out, lhs[0], rhs[1], start=False, stop=False)
                return pe.matmul(out, lhs[1], rhs[0], start=False, stop=stop)

            def transpose_x(p):
                pe.wait_ge(xn_ready, p + 1)
                if p % 2:
                    pe.wait_ge(silu_done, NT * p)
                    pe.wait_ge(hid_ready, NT * p)
                turn_x(p, 0, KT)

            def turn_x(p, first, last_k):
                for k in range(first, last_k):
                    for t in range(HT):
                        last = pe.transpose(ps_xT[k][:, t * P:(t + 1) * P], xn[p % 2][:, t, k * P:(k + 1) * P],
                                            ident[:, :])
                    last.then_inc(xT_done, 1)

            def width_product(out, b, m):
                for k in range(KT):
                    last = product3(out, [w[:, b, m, k * P:(k + 1) * P] for w in (w13_h, w13_l)],
                                    [v[:, k, :] for v in (xT_h, xT_l)], k == 0, k == KT - 1)
                return last

            def gate0(t, b):
                pe.wait_ge(w13_lo, t + 1)
                at_least(pe, silu_done, t - 1)
                width_product(ps_gate[b][:, :], b, 0).then_inc(gate_done, 1)

            def gate_up(i, base, b, first):
                pe.wait_ge(w13_lo, i + (base + NT + 1))
                if not first:
                    at_least(pe, silu_done, i + (base - 1))
                    width_product(ps_gate[b][:, :], b, 0).then_inc(gate_done, 1)
                at_least(pe, hid_ready, i + (base - 1))
                width_product(ps_up[b][:, :], b, 1).then_inc(up_done, 1)

            def down(i, base, b, start, stop):
                pe.wait_ge(w2_lo, i + (base + 1))
                pe.wait_ge(hid_lo, i + (base + 1))
                if start:
                    at_least(pe, x_updated, HT * (base // NT))
                for t in range(HT):
                    last = product3(acc[t][:, :], [h[:, b, t * P:(t + 1) * P] for h in (hid_h, hid_l)],
                                    [w[:, b, :] for w in (w2_h, w2_l)], start, stop)
                last.then_inc(down_done, 1)

            def passes(p, carry_on):
                base, first = NT * p, p == 0
                pe.wait_ge(xT_lo, KT * (p + 1))
                gate_up(0, base, 0, first)
                gate_up(1, base, 1, first)
                down(0, base, 0, True, False)
                with pe.Fori(1, NT // 2) as j:
                    gate_up(j * 2, base, 0, first)
                    down(j * 2 - 1, base, 1, False, False)
                    gate_up(j * 2 + 1, base, 1, first)
                    down(j * 2, base, 0, False, False)
                if carry_on:
                    transpose_x(p + 1)
                if p == 1:
                    first_front()
                down(NT - 1, base, 1, False, True)

            def front_bank(n, f):
                if f >= 3:
                    pe.wait_ge(front_lo, n * FRONT + (f - 2))
                else:
                    at_least(pe, front_lo, n * FRONT)
                return ps_front[f % 3]

            def turn_tokens(n):
                pe.wait_ge(xs_ready, n + 1)
                for f in range(F_X, F_C):
                    dst = front_bank(n, f)
                    for k in range(2):
                        for b in range(ST):
                            last = pe.transpose(dst[:, (k * ST + b) * P:(k * ST + b + 1) * P],
                                                xs[:, b, (2 * f + k) * P:(2 * f + k + 1) * P], ident[:, :])
                    last.then_inc(front_done, 1)

            def conv(n, m, first=0, last=KT):
                dst = front_bank(n, F_C + m) if first == 0 else ps_front[(F_C + m) % 3]
                for k in range(first, last):
                    if m == 0:
                        pe.wait_ge(front_lo, n * FRONT + (F_X + k // 2 + 1))
                    for tap in range(TAPS):
                        ins = product3(dst[:, 0:SEQ], [conv_w(w, tap, k, m) for w in (aw_h, aw_l)],
                                       [v[:, k, tap:tap + SEQ] for v in (xp_h, xp_l)],
                                       k == 0 and tap == 0, k == KT - 1 and tap == TAPS - 1)
                if last == KT:
                    ins.then_inc(front_done, 1)

            def heads_of(n, f):
                c, col = (0, Q_COL) if f < F_K else (1, K_COL)
                pe.wait_ge(front_lo, n * FRONT + (F_C + c + 1))
                dst = front_bank(n, f)
                for e in range(2):
                    m = (f - F_Q) % 4 * 2 + e
                    last = product3(dst[:, e * SEQ:(e + 1) * SEQ], [columns(w, col + m * P, P) for w in (aw_h, aw_l)],
                                    [v[:, c, :] for v in (cT_h, cT_l)], True, True)
                last.then_inc(front_done, 1)

            def turn_values(n):
                pe.wait_ge(front_lo, n * FRONT + (F_C + 3))
                dst = front_bank(n, F_V)
                for b in range(ST):
                    last = pe.transpose(dst[:, b * BLK:(b + 1) * BLK], cv[:, b * BLK:(b + 1) * BLK], ident[:, :])
                last.then_inc(front_done, 1)

            def scores(s, u):
                g, b = u // ST, u % ST
                pe.wait_ge(front_lo, s * FRONT + (F_K + 2 * g + 2))
                for e in range(2):
                    rows, dst = slice(e * DH, (e + 1) * DH), ps_score[e]
                    at_least(pe, exp_done, s * 2 * UNITS + (2 * u + e - 1))
                    pe.matmul(dst[:, :], ident_r[:, :], mask_r[:, :, :].rearrange("p a n -> p (a n)"),
                              start=True, stop=False)
                    for k in range(4):
                        last = product3(dst[:, k * BLK:(k + 1) * BLK],
                                        [v[rows, 4 * g + k, b * BLK:(b + 1) * BLK] for v in (qT_h, qT_l)],
                                        [v[rows, 4 * g + k, b * BLK:(b + 1) * BLK] for v in (kT_h, kT_l)],
                                        False, k == 3)
                    last.then_inc(score_done, 1)

            def turn_probs(s, u):
                pe.wait_ge(norm_done, s * UNITS + (u + 1))
                for e in range(2):
                    if u:
                        pe.wait_ge(z_lo, s * 2 * UNITS + (2 * u + e - 1))
                    for k in range(4):
                        last = pe.transpose(ps_turn[e][:, k * BLK:(k + 1) * BLK],
                                            probs[:, u % 2, (4 * e + k) * BLK:(4 * e + k + 1) * BLK], ident[:, :])
                    last.then_inc(turn_done, 1)

            def attended(s, u):
                if u == 0:
                    pe.wait_ge(front_lo, s * FRONT + FRONT)
                for e in range(2):
                    pe.wait_ge(turn_lo, s * 2 * UNITS + (2 * u + e + 1))
                    product3(ps_turn[e][:, :], [v[:, u % ST, :] for v in (vt_h, vt_l)],
                             [v[:, e, :] for v in (pT_h, pT_l)], True, True).then_inc(z_done, 1)

            def group_output(s, g):
                for e in range(2):
                    pe.wait_ge(z_lo, s * 2 * UNITS + (4 * g + 3 + e))
                    for k in range(4):
                        h = GH * g + 4 * e + k
                        last = product3(ps_y[:, 0:SEQ], [v[:, h, :] for v in (m_h, m_l)],
                                        [v[:, e, k, :, :].rearrange("p b n -> p (b n)") for v in (zT_h, zT_l)],
                                        h == 0, h == HEADS - 1)
                if g:
                    last.then_inc(y_done, 1)

            def project(s):
                pe.wait_ge(y_lo, s + 1)
                for b in range(ST):
                    product3(ps_turn[b][:, :], [v[:, b * BLK:(b + 1) * BLK] for v in (yT_h, yT_l)],
                             [v[:, :] for v in (pw_h, pw_l)], True, True).then_inc(out_done, 1)

            def attend(s, n):
                ahead = n is not None
                if ahead:
                    turn_tokens(n)
                    conv(n, 0)
                scores(s, 1)
                turn_probs(s, 0)
                if ahead:
                    conv(n, 1)
                attended(s, 0)
                if ahead:
                    conv(n, 2, 0, KT // 2)
                scores(s, 2)
                turn_probs(s, 1)
                if ahead:
                    conv(n, 2, KT // 2, KT)
                attended(s, 1)
                if ahead:
                    heads_of(n, F_Q)
                scores(s, 3)
                if ahead:
                    heads_of(n, F_Q + 1)
                turn_probs(s, 2)
                group_output(s, 0)
                attended(s, 2)
                if ahead:
                    for f in range(F_Q + 2, F_K + 2):
                        heads_of(n, f)
                turn_probs(s, 3)
                if ahead:
                    heads_of(n, F_K + 2)
                else:
                    pe.wait_ge(xn_ready, 3)
                    turn_x(2, 0, KT - 1)
                attended(s, 3)
                if ahead:
                    heads_of(n, F_K + 3)
                group_output(s, 1)
                if ahead:
                    scores(n, 0)
                    turn_values(n)
                project(s)

            def first_front():
                pe.wait_ge(silu_done, 2 * NT)
                pe.wait_ge(hid_ready, 2 * NT)
                turn_tokens(0)
                for q in range(4):
                    g, e = q // 2, q % 2
                    rows = slice(e * DH, (e + 1) * DH)
                    pe.wait_ge(mraw_loaded[g], 16)
                    at_least(pe, m_lo, q - 1)
                    for k in range(4):
                        cols = slice(k * W, (k + 1) * W)
                        last = pe.matmul(ps_m[q][:, cols], mraw[g][rows, 0, cols], mraw[g][rows, 1, cols],
                                         start=True, stop=True)
                    last.then_inc(m_done, 1)

            pe.wait_ge(const_ready, 3)
            transpose_x(0)
            pe.wait_ge(tot_ready, 1)
            pe.wait_ge(xT_lo, KT)
            pe.matmul(ps_up[0][:, 0:1], ones[:, :], abs_tot[:, 0:1], start=True, stop=True).then_inc(tot_sum, 1)
            gate0(0, 0)
            gate0(1, 1)
            with pe.Fori(1, NT // 2) as j:
                gate0(j * 2, 0)
                gate0(j * 2 + 1, 1)
            pe.wait_ge(tot_ready, 3)
            pe.matmul(ps_up[0][:, 1:3], ones[:, :], abs_tot[:, 1:3], start=True, stop=True).then_inc(tot_sum, 1)
            passes(0, True)
            passes(1, False)

            pe.wait_ge(m_lo, 4)
            conv(0, 0)
            conv(0, 1)
            pe.wait_ge(small_loaded, 32)
            pe.wait_ge(x_updated, 2 * HT)
            for m in range(MT):
                last = pe.matmul(ps_turn[0][:, 0:1], mraw[m // 4][:, 1, m % 4 * P:(m % 4 + 1) * P],
                                 bias[:, B_V + m:B_V + m + 1], start=m == 0, stop=m == MT - 1)
            last.then_inc(bias_sum, 1)
            conv(0, 2)
            for f in range(F_Q, F_V):
                heads_of(0, f)
            turn_values(0)
            pe.wait_ge(consts_r, 2)
            pe.wait_ge(aw_lo, AW + 1)
            pe.wait_ge(bias_ready, 1)
            scores(0, 0)
            with pe.Fori(0, SEQS - 1) as s:
                attend(s, s + 1)
            attend(SEQS - 1, None)
            turn_x(2, KT - 1, KT)
            passes(2, True)
            passes(3, False)


def kernel(**inputs):
    import numpy as _np
    import concourse.bacc as _bacc
    from concourse.bass_utils import run_bass_kernel_spmd as _run

    a = {n[3:]: _np.asarray(v) for n, v in inputs.items()}

    def inner_cols(w):
        return w.reshape(NT, P, KT, P).transpose(3, 0, 2, 1).reshape(P, NT, DM)

    def inner_rows(w):
        return w.reshape(DM, NT, P).transpose(2, 1, 0)

    def pair(w3, w2):
        return _np.stack([inner_cols(w3), inner_rows(w2)], axis=2).reshape(P, NT * 2 * DM)

    def columns(v):
        return v.reshape(-1, P).T

    wv = a["attn_wv"].transpose(1, 2, 0).reshape(2, MT // 2, P, W)
    wo = a["attn_wo"].reshape(2, MT // 2, P, W)
    attw = [a["attn_conv_w"].reshape(TAPS * KT, P, CONV_OUT).transpose(1, 0, 2), a["attn_wk"], a["attn_wq"],
            a["attn_proj_w"], _np.stack([wv, wo], axis=1).transpose(3, 0, 1, 2, 4)]
    biases = [columns(a["attn_" + n]) for n in ("conv_b", "bq", "bk", "bv", "bo")]
    arrays = {
        "x": a["attn_inputs"].reshape(TOK, DM),
        "w1": inner_cols(a["ffn_w1"]).reshape(P, NT * DM),
        "base1": inner_cols(a["ffn_mean_w1"]).reshape(P, NT * DM),
        "w23": pair(a["ffn_w3"], a["ffn_w2"]),
        "base23": pair(a["ffn_mean_w3"], a["ffn_mean_w2"]),
        "attw": _np.concatenate([v.reshape(P, -1) for v in attw], axis=1),
        "bias": _np.concatenate(biases, axis=1),
        "projb": a["attn_proj_b"],
    }
    arrays = {n: _np.ascontiguousarray(v) for n, v in arrays.items()}
    nc = _bacc.Bacc("TRN2", target_bir_lowering=False, num_devices=1, dynamic_dma_scratch_size=512)
    args = [nc.dram_tensor(n, v.shape, F32, kind="ExternalInput").ap() for n, v in arrays.items()]
    scratch = nc.dram_tensor("formed_weights", (P, NT * 3 * DM), F32, kind="Internal").ap()
    out = nc.dram_tensor("out", (TOK, DM), F32, kind="ExternalOutput").ap()
    macaron(nc, *args, scratch, out)
    r = _run(nc, [arrays], core_ids=[0])
    return r.results[0]["out"].reshape(SEQS, SEQ, DM)
```

```python
from contextlib import ExitStack

import concourse.bass as bass
from concourse import mybir

F32 = mybir.dt.float32
F32R = mybir.dt.float32r
I32 = mybir.dt.int32
I8 = mybir.dt.int8
ALU = mybir.AluOpType
ACT = mybir.ActivationFunctionType
AX_X = mybir.AxisListType.X

P = 128
BANK = 512
TOK = 1024
DM = 512
INTER = 1792
SEQS = 4
SEQ = TOK // SEQS
HALF = 512
KT = DM // P
NT = INTER // P
HT = HALF // P
W = 128
HEADS = 16
DH = 64
HD = HEADS * DH
BLK = 128
TAPS = 3
NEG = -1e30
EPS = 1e-5
RSQRT_MAGIC = float(0x5F3759DF)
RING = 4
CH1 = NT // 2
DIFF_DVE = (5, 6)
PREFETCH = 2
SCALE = DH ** -0.5
CONV_OUT = 3 * W
AW = TAPS * KT * CONV_OUT // BANK + 2 * HD // BANK
ST = SEQ // P
MT = HD // P
GH = 8
UNITS = ST * HEADS // GH
B_CONV, B_Q, B_K, B_V, B_O = 0, 3, 3 + MT, 3 + 2 * MT, 3 + 3 * MT
TURNED = 2
CONV = (2, 5, 8)
F_CV = CONV[2]
HEADS_IN = {3: (0, 0), 4: (0, 2), 6: (1, 0), 7: (1, 2), 9: (0, 4), 10: (0, 6), 11: (1, 4), 12: (1, 6)}
KEYS_OF = {m: f for f, (keys, m) in HEADS_IN.items() if keys}
F_V, FRONT = 13, 14


def at_least(eng, sem, value):
    if not (isinstance(value, int) and value <= 0):
        eng.wait_ge(sem, value)


def macaron(nc, x_in, w_in, base_in, attw_in, bias_in, projb_in, scratch, out):
    with ExitStack() as ctx:
        def at(name, shape, offset, dt=F32):
            return nc.alloc_sbuf_tensor_at(name, [P] + shape, dt, offset=offset)

        def sem(name):
            return ctx.enter_context(nc.semaphore(name))

        COMMON = 640
        x = at("x", [TOK // P, DM], COMMON)
        o = COMMON + 4 * TOK // P * DM
        ident = at("ident", [P], o)
        ones = at("ones", [P], o + 512)
        stats = at("stats", [HT, 6], o + 1024)
        newton = at("newton", [HT], o + 1120)
        varep = at("varep", [HT], o + 1152)
        mv = at("mv", [2 * HT, 2], o + 1184)
        rstd = at("rstd", [2 * HT], o + 1504)
        abs_sum = at("abs_sum", [3, NT], o + 1248)
        abs_tot = at("abs_tot", [3], o + 1440)
        coeff = at("coeff", [3], o + 1472)
        ident_r = at("ident_r", [P], o + 1536, F32R)
        mask_r = at("mask_r", [4, BLK], o + 2048, F32R)
        projb = at("projb", [DM], o + 4096)
        bias = at("bias", [B_O + 1], o + 6144)
        o = COMMON + 22656
        w13_h = at("w13_h", [2, 2, 512], o, F32R)
        w13_l = at("w13_l", [2, 2, 512], o + 8192, F32R)
        w2_h = at("w2_h", [2, DM], o + 16384, F32R)
        w2_l = at("w2_l", [2, DM], o + 20480, F32R)
        hid = at("hid", [2, HALF], o + 24576)
        hid_h = at("hid_h", [2, HALF], o + 28672, F32R)
        hid_l = at("hid_l", [2, HALF], o + 32768, F32R)
        xT_h = at("xT_h", [KT, HALF], o + 36864, F32R)
        xT_l = at("xT_l", [KT, HALF], o + 45056, F32R)
        WTS = o + 53248
        wts = at("wts", [3, NT, 512], WTS)
        R3 = WTS + 4 * NT * 3 * 512
        sgn = at("sgn", [3, NT, 512], R3, I8)
        gates = at("gates", [NT, HALF], R3 + 21504)
        raw = at("raw", [RING, 1024], R3 + 50176)
        xn = [at(f"xn_{p}", [HT, DM], R3 + place)
              for p, place in enumerate((21504, 57344, 57344, 21504))]

        mask_f = at("mask_f", [4, BLK], R3 + 21504 + 4 * 512 * (NT - 1))

        aw_h = at("aw_h", [AW, BANK], R3, F32R)
        aw_l = at("aw_l", [AW, BANK], R3 + 26624, F32R)
        aw_raw = at("aw_raw", [2, BANK], R3 + 53248)
        a = COMMON + 22656
        probs = at("probs", [2, GH * BLK], a)
        pT_h = at("pT_h", [2, 4 * BLK], a + 8192, F32R)
        pT_l = at("pT_l", [2, 4 * BLK], a + 12288, F32R)
        pw_h = at("pw_h", [DM], a + 16384, F32R)
        pw_l = at("pw_l", [DM], a + 18432, F32R)
        qT_h = at("qT_h", [MT, SEQ], a + 20480, F32R)
        qT_l = at("qT_l", [MT, SEQ], a + 28672, F32R)
        k_places = [(a + 36864, a + 45056)]
        a, b, c = (WTS + (m * NT + PREFETCH) * 2048 for m in range(3))
        xp_h = at("xp_h", [KT, SEQ + 2], a, F32R)
        xp_l = at("xp_l", [KT, SEQ + 2], a + 4128, F32R)
        mraw = [at("mraw_0", [2, BANK], R3 + 61440), at("mraw_1", [2, BANK], a + 8256)]
        cT_h = at("cT_h", [2, SEQ], a + 12352, F32R)
        cT_l = at("cT_l", [2, SEQ], a + 14400, F32R)
        cv = at("cv", [SEQ], a + 16448)
        vt_h = at("vt_h", [ST, W], a + 17472, F32R)
        vt_l = at("vt_l", [ST, W], a + 18496, F32R)
        m_h = at("m_h", [HEADS, W], b, F32R)
        m_l = at("m_l", [HEADS, W], b + 8192, F32R)
        yT_h = at("yT_h", [SEQ], a + 19520, F32R)
        yT_l = at("yT_l", [SEQ], a + 20544, F32R)
        row_max = at("row_max", [2, GH], a + 21568)
        neg_max = at("neg_max", [2, GH], a + 21632)
        row_sum = at("row_sum", [2, GH], a + 21696)
        inv_sum = at("inv_sum", [2, GH], a + 21760)
        out_bias = at("out_bias", [1], a + 21824)
        zT_h = at("zT_h", [2, 4, ST, BLK], c, F32R)
        zT_l = at("zT_l", [2, 4, ST, BLK], c + 8192, F32R)
        k_places.append((b + 16384, c + 16384))
        kT_h = [at(f"kT_h{g}", [MT // 2, ST, 2, BLK], k_places[g][0], F32R) for g in range(2)]
        kT_l = [at(f"kT_l{g}", [MT // 2, ST, 2, BLK], k_places[g][1], F32R) for g in range(2)]
        xs = at("xs", [ST, DM], R3 + 57344)

        def columns(part, first, n):
            return part[:, :, :].rearrange("p c n -> p (c n)")[:, first:first + n]

        def conv_w(part, tap, k, m):
            return columns(part, (tap * KT + k) * CONV_OUT + m * W, W)

        K_COL = TAPS * KT * CONV_OUT
        Q_COL = K_COL + HD

        bank = [ctx.enter_context(nc.psum_tensor(f"bank{i}", [P, BANK], F32)) for i in range(8)]
        ps_gate, ps_up, acc = bank[0:2], bank[2:4], bank[4:8]
        ps_xT = bank[0:4]
        ps_total = bank[4]
        ps_front, ps_y, ps_turn, ps_score = bank[0:3], bank[3], bank[4:6], bank[6:8]
        ps_m = [bank[2], bank[3], bank[2], bank[3]]

        x_loaded = [sem("x_loaded_a"), sem("x_loaded_b")]
        raw_loaded = [sem(f"raw_loaded{i}") for i in range(RING)]
        diff_done = sem("diff_done")
        dve_diff = sem("dve_diff")
        sign_done = sem("sign_done")
        abs_done = sem("abs_done")
        tot_ready = sem("tot_ready")
        tot_sum = sem("tot_sum")
        const_ready = sem("const_ready")
        dve_chain = sem("dve_chain")
        xn_ready = sem("xn_ready")
        xT_done = sem("xT_done")
        xT_hi = sem("xT_hi")
        xT_lo = sem("xT_lo")
        w1_formed = sem("w1_formed")
        w3_formed = sem("w3_formed")
        w2_formed = sem("w2_formed")
        w13_hi = sem("w13_hi")
        w13_lo = sem("w13_lo")
        w2_hi = sem("w2_hi")
        w2_lo = sem("w2_lo")
        early_done = sem("early_done")
        gate_done = sem("gate_done")
        up_done = sem("up_done")
        down_done = sem("down_done")
        down_tile = sem("down_tile")
        silu_done = sem("silu_done")
        hid_ready = sem("hid_ready")
        hid_hi = sem("hid_hi")
        hid_lo = sem("hid_lo")
        x_updated = sem("x_updated")
        w_saved = sem("w_saved")
        w_loaded = [sem("w_loaded_even"), sem("w_loaded_odd")]
        stored = sem("stored")
        small_loaded = sem("small_loaded")
        mask_ready = sem("mask_ready")
        consts_r = sem("consts_r")
        aw_loaded = [sem("aw_loaded_even"), sem("aw_loaded_odd")]
        aw_hi = sem("aw_hi")
        aw_lo = sem("aw_lo")
        mraw_loaded = [sem("mraw_loaded_0"), sem("mraw_loaded_1")]
        m_done = sem("m_done")
        m_hi = sem("m_hi")
        m_lo = sem("m_lo")
        bias_sum = sem("bias_sum")
        bias_ready = sem("bias_ready")
        xs_ready = sem("xs_ready")
        x_biased = sem("x_biased")
        zeros_ready = sem("zeros_ready")
        front_done = sem("front_done")
        front_hi = sem("front_hi")
        front_lo = sem("front_lo")
        score_done = sem("score_done")
        max_found = sem("max_found")
        max_ready = sem("max_ready")
        exp_done = sem("exp_done")
        sum_inverted = sem("sum_inverted")
        norm_done = sem("norm_done")
        turn_done = sem("turn_done")
        turn_hi = sem("turn_hi")
        turn_lo = sem("turn_lo")
        z_done = sem("z_done")
        z_hi = sem("z_hi")
        z_lo = sem("z_lo")
        y_done = sem("y_done")
        y_hi = sem("y_hi")
        y_lo = sem("y_lo")
        out_done = sem("out_done")
        x_attended = sem("x_attended")

        def chunk_slot(k):
            return k % RING, k // RING + 1

        def pool_diffs(k):
            return k + 1 - sum(1 for c in DIFF_DVE if c < k)

        def ring_steps(eng, body):
            for t in range(4):
                body(t, t, 0)
            with eng.Fori(0, (NT - 6) // 4) as j:
                for q in range(4):
                    body(j * 4 + (4 + q), 4 + q, j)
            for t in range(NT - 2, NT):
                body(t, t, 0)

        def tile_of(m, i):
            return wts[:, m, bass.ds(i, 1), :].rearrange("p a n -> p (a n)")

        def small_chunk(m, tt, j):
            k = CH1 + (m - 1) * NT + tt
            return k % RING, j + (k // RING + 1)

        def before(m):
            return CH1 + (m - 1) * NT

        head_rows = [slice(0, DH), slice(DH, P)]

        def key_place(parts, m, rows):
            return parts[m // 4][rows, m % 4, :, rows.start // DH, :]

        def score_bank(s, u, i):
            return ps_front[i] if isinstance(s, int) and s == SEQS - 1 and u % 2 else ps_score[i]

        def m_place(part, q):
            group = part[:, GH * (q // 2):GH * (q // 2 + 1), :].rearrange("p (k e) n -> p k e n", e=2)
            return group[:, :, q % 2, :]

        def split_of(f):
            return f + 1 if f < F_CV else f

        block = ctx.enter_context(nc.Block())

        @block.sync
        def _(sp):
            def load_chunk1(k):
                at_least(sp, abs_done, k - RING + 1)
                at_least(sp, sign_done, k - RING + 1)
                slot, _ = chunk_slot(k)
                sp.dma_start(raw[:, slot, :], w_in[:, 1024 * k:1024 * (k + 1)]).then_inc(raw_loaded[slot], 16)
                sp.dma_start(wts[:, 0, 2 * k:2 * k + 2, :].rearrange("p t n -> p (t n)"),
                             base_in[:, 1024 * k:1024 * (k + 1)]).then_inc(raw_loaded[slot], 16)

            def load_small_chunk(m, t, tt, j):
                if m == 1:
                    at_least(sp, abs_done, t + (before(m) - RING + 1))
                at_least(sp, sign_done, t + (before(m) - RING + 1))
                slot, _ = small_chunk(m, tt, j)
                cols = bass.ds(t * 512 + m * NT * 512, 512)
                sp.dma_start(raw[:, slot, 0:512], w_in[:, cols]).then_inc(raw_loaded[slot], 16)
                sp.dma_start(tile_of(m, t), base_in[:, cols]).then_inc(raw_loaded[slot], 16)

            def load_attw_chunk(c, slot):
                at_least(sp, aw_hi, c - 1)
                at_least(sp, aw_lo, c - 1)
                sp.dma_start(aw_raw[:, slot, :], attw_in[:, bass.ds(c * BANK, BANK)]).then_inc(aw_loaded[slot], 16)

            def load_attw(c0, c1, first):
                if first:
                    sp.wait_ge(sign_done, before(3))
                for c in range(c0, c0 + 2):
                    load_attw_chunk(c, c % 2)
                with sp.Fori(1, (c1 - c0) // 2) as j:
                    for q in range(2):
                        load_attw_chunk(j * 2 + (c0 + q), (c0 + q) % 2)
                if (c1 - c0) % 2:
                    load_attw_chunk(c1 - 1, (c1 - 1) % 2)

            def load_formed(i, slot, j):
                at_least(sp, w_loaded[slot], j * 16)
                sp.dma_start(wts[:, :, bass.ds(i, 1), :].rearrange("p a b n -> p a (b n)"),
                             scratch[:, bass.ds(i * 1536, 1536)].rearrange("p (a n) -> p a n", a=3)
                             ).then_inc(w_loaded[slot], 16)

            xv = x_in.rearrange("(t p) d -> p t d", p=P)
            sp.dma_start(x[:, 0:HT, :], xv[:, 0:HT, :]).then_inc(x_loaded[0], 16)
            for k in range(CH1):
                load_chunk1(k)
            sp.dma_start(x[:, HT:2 * HT, :], xv[:, HT:2 * HT, :]).then_inc(x_loaded[1], 16)
            ring_steps(sp, lambda t, tt, j: load_small_chunk(1, t, tt, j))
            sp.dma_start(bias[:, :], bias_in).then_inc(small_loaded, 16)
            sp.dma_start(projb[:, :], projb_in.partition_broadcast(P)).then_inc(small_loaded, 16)
            sp.wait_ge(abs_done, before(2))
            ring_steps(sp, lambda t, tt, j: load_small_chunk(2, t, tt, j))
            with sp.Fori(0, NT) as i:
                sp.wait_ge(w2_formed, i + 1)
                sp.dma_start(scratch[:, bass.ds(i * 1536, 1536)].rearrange("p (a n) -> p a n", a=3),
                             wts[:, :, bass.ds(i, 1), :].rearrange("p a b n -> p a (b n)")).then_inc(w_saved, 16)
            load_attw(0, AW + 1, True)
            for g in range(2):
                if g:
                    sp.wait_ge(w_saved, 16 * NT)
                    sp.wait_ge(w2_lo, 2 * NT)
                sp.dma_start(mraw[g][:, :, :].rearrange("p a n -> p (a n)"),
                             attw_in[:, (AW + 1 + 2 * g) * BANK:(AW + 3 + 2 * g) * BANK]).then_inc(mraw_loaded[g], 16)
            for i in range(PREFETCH):
                load_formed(i, i % 2, i // 2)
            sp.wait_ge(x_attended, 2 * HT)
            with sp.Fori(PREFETCH // 2, NT // 2) as j:
                for q in range(2):
                    load_formed(j * 2 + q, q, j)
            for t in range(2 * HT):
                sp.wait_ge(x_updated, 2 * HT + t + 1)
                sp.dma_start(out[t * P:(t + 1) * P, :], x[:, t, :]).then_inc(stored, 16)
            sp.wait_ge(stored, 16 * 2 * HT)

        @block.gpsimd
        def _(pool):
            pool.memset(ident[:, :], 0.0).then_inc(const_ready, 1)
            pool.memset(ones[:, :], 1.0).then_inc(const_ready, 1)
            pool.wait_ge(const_ready, 2)
            pool.affine_select(out=ident[:, :], in_=ident[:, :], compare_op=ALU.not_equal, fill=1.0,
                               base=0, pattern=[[-1, P]], channel_multiplier=1).then_inc(const_ready, 1)
            pool.memset(mask_f[:, :, :], 0.0).then_inc(mask_ready, 1)
            pool.wait_ge(mask_ready, 1)
            pool.affine_select(out=mask_f[:, :, :], in_=mask_f[:, :, :], compare_op=ALU.is_ge, fill=NEG,
                               base=0, pattern=[[0, 4], [-1, BLK]], channel_multiplier=1).then_inc(mask_ready, 1)

            for k in range(CH1):
                if k not in DIFF_DVE:
                    slot, use = chunk_slot(k)
                    pool.wait_ge(raw_loaded[slot], 32 * use)
                    r = raw[:, slot, :].rearrange("p (t n) -> p t n", t=2)
                    pool.tensor_tensor(r, r, wts[:, 0, 2 * k:2 * k + 2, :], ALU.subtract).then_inc(diff_done, 1)

            def small_diff(m, t, tt, j):
                slot, use = small_chunk(m, tt, j)
                pool.wait_ge(raw_loaded[slot], use * 32)
                pool.tensor_tensor(raw[:, slot, 0:512], raw[:, slot, 0:512], tile_of(m, t),
                                   ALU.subtract).then_inc(diff_done, 1)

            for m in (1, 2):
                ring_steps(pool, lambda t, tt, j: small_diff(m, t, tt, j))

            pool.wait_ge(w_saved, 16 * NT)
            pool.wait_ge(w2_lo, 2 * NT)
            pool.wait_ge(down_done, 2 * NT)
            for part in (kT_h[0], kT_l[0], kT_h[1], kT_l[1]):
                for e in range(2):
                    rows = slice(e * DH, (e + 1) * DH)
                    pool.memset(part[rows, :, :, 1 - e, :].bitcast(F32), 0.0).then_inc(zeros_ready, 1)
            pool.wait_ge(zeros_ready, 8)

            pool.wait_ge(small_loaded, 32)
            with pool.Fori(0, SEQS) as s:
                pool.wait_ge(xs_ready, s + 1)
                for t in range(ST):
                    tile = x[:, bass.ds(s * ST + t, 1), :].rearrange("p a n -> p (a n)")
                    pool.tensor_tensor(tile, tile, projb[:, :], ALU.add).then_inc(x_biased, 1)

        @block.scalar
        def _(act):
            def sign1(k):
                if k in DIFF_DVE:
                    act.wait_ge(dve_diff, DIFF_DVE.index(k) + 1)
                else:
                    act.wait_ge(diff_done, pool_diffs(k))
                slot, _ = chunk_slot(k)
                act.activation(sgn[:, 0, 2 * k:2 * k + 2, :],
                               raw[:, slot, :].rearrange("p (t n) -> p t n", t=2), ACT.Sign).then_inc(sign_done, 1)

            def small_sign(m, t, tt, j):
                act.wait_ge(diff_done, t + (before(m) - len(DIFF_DVE) + 1))
                r = raw[:, small_chunk(m, tt, j)[0], 0:512]
                ins = act.activation(sgn[:, m, bass.ds(t, 1), :].rearrange("p a n -> p (a n)"), r, ACT.Sign)
                if m == 2:
                    ins = act.activation(r, r, ACT.Abs, accum_out=abs_sum[:, 2, bass.ds(t, 1)])
                ins.then_inc(sign_done, 1)

            def xT_high(p, first=0, last=KT):
                for k in range(first, last):
                    act.wait_ge(xT_done, KT * p + k + 1)
                    act.activation(xT_h[:, k, :], ps_xT[k][:, :], ACT.Copy).then_inc(xT_hi, 1)

            def early_high(m, t, tt):
                n = m * NT + tt
                act.wait_ge((w1_formed, w3_formed)[m], t + 1)
                at_least(act, early_done, t + (m * NT - 3))
                act.activation(w13_h[:, n % 2, n // 2 % 2, :], tile_of(m, t), ACT.Copy).then_inc(w13_hi, 1)

            def silu_store(t, tt):
                act.wait_ge(early_done, t + 1)
                act.activation(gates[:, bass.ds(t, 1), :].rearrange("p a n -> p (a n)"), bank[tt % 4][:, :],
                               ACT.Silu).then_inc(silu_done, 1)

            def w13_high(i, base, b):
                at_least(act, up_done, i + (base - NT - 1))
                act.activation(w13_h[:, b, :, :], wts[:, 0:2, bass.ds(i, 1), :].rearrange("p a b n -> p a (b n)"),
                               ACT.Copy).then_inc(w13_hi, 1)

            def w2_high(i, base, b, first):
                if first:
                    act.wait_ge(w2_formed, i + 1)
                at_least(act, down_done, i + (base - 1))
                act.activation(w2_h[:, b, :], tile_of(2, i), ACT.Copy).then_inc(w2_hi, 1)

            def hid_high(i, base, b, first):
                act.wait_ge(hid_ready, i + (base + 1))
                at_least(act, down_done, i + (base - 1))
                src = gates[:, bass.ds(i, 1), :].rearrange("p a n -> p (a n)") if first else hid[:, b, :]
                act.activation(hid_h[:, b, :], src, ACT.Copy).then_inc(hid_hi, 1)

            def silu(i, base, b):
                act.wait_ge(gate_done, i + (base - NT + 1))
                at_least(act, hid_lo, i + (base - 1))
                act.activation(hid[:, b, :], ps_gate[b][:, :], ACT.Silu).then_inc(silu_done, 1)

            def attw_high(c, slot, use):
                act.wait_ge(aw_loaded[slot], use * 16)
                act.activation(aw_h[:, bass.ds(c, 1), :].rearrange("p a n -> p (a n)"), aw_raw[:, slot, :],
                               ACT.Copy).then_inc(aw_hi, 1)

            def step(i, base, b, pair, split=True):
                if split:
                    if base == 2 * NT:
                        act.wait_ge(w_loaded[b], pair * 16 + 16)
                    w13_high(i, base, b)
                if base == NT:
                    attw_high(i - 1, 1 - b, pair + b)
                silu(i - 1, base, 1 - b)
                hid_high(i - 1, base, 1 - b, False)
                w2_high(i, base, b, False)

            def passes(p, carry_on):
                base = NT * p
                step(1, base, 1, 0, False)
                with act.Fori(1, NT // 2) as j:
                    step(j * 2, base, 0, j)
                    step(j * 2 + 1, base, 1, j)
                if carry_on:
                    w13_high(0, base + NT, 0)
                silu(NT - 1, base, 1)
                hid_high(NT - 1, base, 1, False)
                if carry_on:
                    next_half(p + 1)

            def next_half(p):
                w2_high(0, NT * p, 0, False)
                xT_high(p)
                w13_high(1, NT * p, 1)

            act.wait_ge(const_ready, 3)
            act.activation(ident_r[:, :], ident[:, :], ACT.Copy).then_inc(consts_r, 1)
            act.wait_ge(mask_ready, 2)
            act.activation(mask_r[:, :, :], mask_f[:, :, :], ACT.Copy).then_inc(consts_r, 1)
            for k in range(CH1):
                sign1(k)
                if k == 2:
                    xT_high(0)

            def gate_step(t, tt, j):
                early_high(0, t, tt)
                small_sign(1, t, tt, j)
                if tt >= 2:
                    silu_store(t - 2, tt - 2)

            def up_step(t, tt, j):
                early_high(1, t, tt)
                if isinstance(t, int) and t < 2:
                    silu_store(NT - 2 + t, NT - 2 + t)
                small_sign(2, t, tt, j)

            ring_steps(act, gate_step)
            ring_steps(act, up_step)

            def down_step(i, b):
                hid_high(i, 0, b, True)
                w2_high(i, 0, b, True)

            down_step(0, 0)
            down_step(1, 1)
            with act.Fori(1, NT // 2) as j:
                down_step(j * 2, 0)
                down_step(j * 2 + 1, 1)
            act.wait_ge(early_done, 2 * NT)
            w13_high(0, NT, 0)
            next_half(1)
            act.wait_ge(hid_lo, NT)
            passes(1, False)

            def high(out, in_, bias_column=None):
                if bias_column is None:
                    return act.activation(out, in_, ACT.Copy)
                return act.activation(out, in_, ACT.Identity, bias=bias_column)

            def front(n, f):
                act.wait_ge(front_done, n * FRONT + (f + 1))
                src = ps_front[f % 3]
                if f < TURNED:
                    ins = high(xp_h[:, 2 * f:2 * f + 2, 1:SEQ + 1], src[:, :].rearrange("p (k n) -> p k n", k=2))
                elif f in CONV:
                    m = CONV.index(f)
                    ins = high(cT_h[:, m, :], src[:, 0:SEQ], bias[:, B_CONV + m:B_CONV + m + 1])
                elif f in HEADS_IN:
                    keys, m0 = HEADS_IN[f]
                    for t in range(2):
                        m, cols = m0 + t, slice(t * SEQ, (t + 1) * SEQ)
                        if not keys:
                            ins = high(qT_h[:, m, :], src[:, cols], bias[:, B_Q + m:B_Q + m + 1])
                        else:
                            for rows in head_rows:
                                ins = high(key_place(kT_h, m, rows),
                                           src[rows, cols].rearrange("p (b n) -> p b n", b=ST),
                                           bias[rows, B_K + m:B_K + m + 1])
                else:
                    ins = high(vt_h[:, :, :].rearrange("p b n -> p (b n)"), src[:, 0:SEQ])
                ins.then_inc(front_hi, 1)

            def exps(s, u, banks=(0, 1)):
                act.wait_ge(max_ready, s * UNITS + (u + 1))
                for e in banks:
                    for k in range(4):
                        h = 4 * e + k
                        ins = act.activation(probs[:, u % 2, h * BLK:(h + 1) * BLK],
                                             score_bank(s, u, e)[:, k * BLK:(k + 1) * BLK], ACT.Exp,
                                             bias=neg_max[:, u % 2, h:h + 1], scale=SCALE,
                                             accum_out=row_sum[:, u % 2, h:h + 1])
                    ins.then_inc(exp_done, 1)

            def probs_high(s, u):
                for e in range(2):
                    act.wait_ge(turn_done, s * 2 * UNITS + (2 * u + e + 1))
                    high(pT_h[:, e, :], ps_turn[e][:, :]).then_inc(turn_hi, 1)

            def z_high(s, u):
                for e in range(2):
                    act.wait_ge(z_done, s * 2 * UNITS + (2 * u + e + 1))
                    high(zT_h[:, e, :, u % ST, :],
                         ps_turn[e][:, :].rearrange("p (k n) -> p k n", k=4)).then_inc(z_hi, 1)

            def y_high(s):
                act.wait_ge(y_done, s + 1)
                high(yT_h[:, :], ps_y[:, 0:SEQ], out_bias[:, :]).then_inc(y_hi, 1)

            def attend(s, n, after):
                def fronts(first, last):
                    for f in range(first, last):
                        if f != F_CV:
                            front(n, f)

                exps(s, 0)
                fronts(2, 3)
                probs_high(s, 0)
                exps(s, 1)
                fronts(3, 5)
                z_high(s, 0)
                fronts(5, 7)
                probs_high(s, 1)
                exps(s, 2)
                z_high(s, 1)
                fronts(7, 8)
                exps(s, 3)
                probs_high(s, 2)
                fronts(9, 10)
                z_high(s, 2)
                fronts(10, 11)
                probs_high(s, 3)
                fronts(11, 13)
                z_high(s, 3)
                fronts(F_V, FRONT)
                y_high(s)
                if after is not None:
                    for f in range(TURNED):
                        front(after, f)

            def attend_last(s):
                exps(s, 0)
                exps(s, 1)
                probs_high(s, 0)
                exps(s, 2, (0,))
                z_high(s, 0)
                exps(s, 2, (1,))
                probs_high(s, 1)
                exps(s, 3, (0,))
                z_high(s, 1)
                exps(s, 3, (1,))
                probs_high(s, 2)
                z_high(s, 2)
                probs_high(s, 3)
                xT_high(2, 0, KT - 1)
                z_high(s, 3)
                y_high(s)

            act.wait_ge(w_saved, 16 * NT)
            act.wait_ge(w2_lo, 2 * NT)
            act.wait_ge(small_loaded, 32)
            for f in range(TURNED):
                front(0, f)
            for q in range(4):
                act.wait_ge(m_done, q + 1)
                high(m_place(m_h, q), ps_m[q][:, :].rearrange("p (k n) -> p k n", k=4)).then_inc(m_hi, 1)
            act.wait_ge(down_done, 2 * NT)
            act.wait_ge(aw_loaded[AW % 2], 16 * (AW // 2 + 1))
            high(pw_h[:, :], aw_raw[:, AW % 2, :]).then_inc(aw_hi, 1)
            for f in range(TURNED, FRONT):
                if f != F_CV:
                    front(0, f)
            for f in range(TURNED):
                front(1, f)
            act.wait_ge(bias_ready, 1)
            with act.Fori(0, SEQS - 2) as s:
                attend(s, s + 1, s + 2)
            attend(SEQS - 2, SEQS - 1, None)
            attend_last(SEQS - 1)

            act.wait_ge(w_loaded[0], 16)
            w13_high(0, 2 * NT, 0)
            xT_high(2, KT - 1)
            act.wait_ge(x_attended, 2 * HT)
            w2_high(0, 2 * NT, 0, False)
            act.wait_ge(w_loaded[1], 16)
            w13_high(1, 2 * NT, 1)
            passes(2, True)
            passes(3, False)

        @block.vector
        def _(dve):
            chain = [0]

            def link(ins):
                chain[0] += 1
                ins.then_inc(dve_chain, 1)
                dve.wait_ge(dve_chain, chain[0])

            def norm_sums(p):
                for t in range(HT):
                    last = dve.bn_stats(stats[:, t, :], x[:, HT * p + t, :])
                link(last)

            def norm_stats(p):
                half = slice(HT * p, HT * (p + 1))
                v, r, w = varep[:, :], rstd[:, half], newton[:, :]
                dve.memset(v, EPS)
                for t in range(HT):
                    last = dve.bn_aggr(mv[:, HT * p + t, :], stats[:, t, :])
                link(last)
                link(dve.tensor_tensor(v, mv[:, half, 1], v, ALU.add))
                link(dve.tensor_scalar(r.bitcast(I32), v.bitcast(I32), -0.5, RSQRT_MAGIC, ALU.mult, ALU.add))
                for _ in range(3):
                    link(dve.scalar_tensor_tensor(out=w, in0=r, scalar=-0.5, in1=r, op0=ALU.mult, op1=ALU.mult))
                    link(dve.tensor_tensor(w, w, v, ALU.mult))
                    link(dve.scalar_tensor_tensor(out=r, in0=w, scalar=1.5, in1=r, op0=ALU.add, op1=ALU.mult))

            def normalise(p, first=0, last=HT):
                for t in range(first, last):
                    i = HT * p % (2 * HT) + t
                    ins = dve.tensor_scalar(xn[p][:, t, :], x[:, i, :], mv[:, i, 0:1], rstd[:, i:i + 1],
                                            ALU.subtract, ALU.mult)
                if last == HT:
                    ins.then_inc(xn_ready, 1)

            def xT_low(p, first=0, last=KT):
                for k in range(first, last):
                    dve.wait_ge(xT_hi, KT * p + k + 1)
                    dve.tensor_tensor(xT_l[:, k, :], ps_xT[k][:, :], xT_h[:, k, :].bitcast(F32),
                                      ALU.subtract).then_inc(xT_lo, 1)

            def sum_abs1(k):
                slot, use = chunk_slot(k)
                if k in DIFF_DVE:
                    dve.wait_ge(raw_loaded[slot], 32 * use)
                    r = raw[:, slot, :].rearrange("p (t n) -> p t n", t=2)
                    dve.tensor_tensor(r, r, wts[:, 0, 2 * k:2 * k + 2, :], ALU.subtract).then_inc(dve_diff, 1)
                    dve.wait_ge(dve_diff, DIFF_DVE.index(k) + 1)
                else:
                    dve.wait_ge(diff_done, pool_diffs(k))
                dve.tensor_reduce(abs_sum[:, 0, k:k + 1], raw[:, slot, :], AX_X, ALU.add,
                                  apply_absolute_value=True).then_inc(abs_done, 1)

            def small_sum(t, tt, j):
                dve.wait_ge(diff_done, t + (before(1) - len(DIFF_DVE) + 1))
                dve.tensor_reduce(abs_sum[:, 1, bass.ds(t, 1)], raw[:, small_chunk(1, tt, j)[0], 0:512],
                                  AX_X, ALU.add, apply_absolute_value=True).then_inc(abs_done, 1)

            def form(m, i, done):
                dve.scalar_tensor_tensor(out=tile_of(m, i),
                                         in0=sgn[:, m, bass.ds(i, 1), :].rearrange("p a n -> p (a n)"),
                                         scalar=coeff[:, m:m + 1], in1=tile_of(m, i), op0=ALU.mult,
                                         op1=ALU.add).then_inc(done, 1)

            def early_low(m, t, tt):
                n = m * NT + tt
                dve.wait_ge(w13_hi, t + (m * NT + 1))
                at_least(dve, early_done, t + (m * NT - 3))
                dve.tensor_tensor(w13_l[:, n % 2, n // 2 % 2, :], tile_of(m, t),
                                  w13_h[:, n % 2, n // 2 % 2, :].bitcast(F32), ALU.subtract).then_inc(w13_lo, 1)

            def w13_low(i, base, b):
                dve.wait_ge(w13_hi, i + (base + NT + 1))
                dve.tensor_tensor(w13_l[:, b, :, :], wts[:, 0:2, bass.ds(i, 1), :].rearrange("p a b n -> p a (b n)"),
                                  w13_h[:, b, :, :].bitcast(F32), ALU.subtract).then_inc(w13_lo, 1)

            def w2_low(i, base, b):
                dve.wait_ge(w2_hi, i + (base + 1))
                dve.tensor_tensor(w2_l[:, b, :], tile_of(2, i),
                                  w2_h[:, b, :].bitcast(F32), ALU.subtract).then_inc(w2_lo, 1)

            def hidden_early(t, tt):
                dve.wait_ge(silu_done, t + 1)
                dve.wait_ge(early_done, t + (NT + 1))
                h = gates[:, bass.ds(t, 1), :].rearrange("p a n -> p (a n)")
                dve.tensor_tensor(h, h, bank[(NT + tt) % 4][:, :], ALU.mult).then_inc(hid_ready, 1)

            def hidden_early_low(i, b):
                dve.wait_ge(hid_hi, i + 1)
                dve.tensor_tensor(hid_l[:, b, :], gates[:, bass.ds(i, 1), :].rearrange("p a n -> p (a n)"),
                                  hid_h[:, b, :].bitcast(F32), ALU.subtract).then_inc(hid_lo, 1)

            def hidden(i, base, b):
                dve.wait_ge(silu_done, i + (base + 1))
                dve.wait_ge(up_done, i + (base - NT + 1))
                h = hid[:, b, :]
                dve.tensor_tensor(h, h, ps_up[b][:, :], ALU.mult).then_inc(hid_ready, 1)
                dve.wait_ge(hid_hi, i + (base + 1))
                dve.tensor_tensor(hid_l[:, b, :], h, hid_h[:, b, :].bitcast(F32), ALU.subtract).then_inc(hid_lo, 1)

            def attw_low(c, slot):
                dve.wait_ge(aw_hi, c + 1)
                high, low = (v[:, bass.ds(c, 1), :].rearrange("p a n -> p (a n)") for v in (aw_h, aw_l))
                dve.tensor_tensor(low, aw_raw[:, slot, :], high.bitcast(F32), ALU.subtract).then_inc(aw_lo, 1)

            def low(out, in_, high, bias_column=None):
                if bias_column is None:
                    return dve.tensor_tensor(out, in_, high.bitcast(F32), ALU.subtract)
                return dve.scalar_tensor_tensor(out=out, in0=in_, scalar=bias_column, in1=high.bitcast(F32),
                                                op0=ALU.add, op1=ALU.subtract)

            def sequence_norm(n):
                for t in range(ST):
                    i = bass.ds(n * ST + t, 1)
                    ins = dve.tensor_scalar(xs[:, t, :], x[:, i, :].rearrange("p a n -> p (a n)"),
                                            mv[:, i, 0:1].rearrange("p a n -> p (a n)"), rstd[:, i],
                                            ALU.subtract, ALU.mult)
                ins.then_inc(xs_ready, 1)

            def front(n, f):
                if f == F_CV:
                    dve.wait_ge(front_done, n * FRONT + (f + 1))
                else:
                    dve.wait_ge(front_hi, n * (FRONT - 1) + split_of(f))
                src = ps_front[f % 3]
                if f < TURNED:
                    ins = low(xp_l[:, 2 * f:2 * f + 2, 1:SEQ + 1], src[:, :].rearrange("p (k n) -> p k n", k=2),
                              xp_h[:, 2 * f:2 * f + 2, 1:SEQ + 1])
                elif f == F_CV:
                    ins = dve.tensor_scalar(cv[:, :], src[:, 0:SEQ], bias[:, B_CONV + 2:B_CONV + 3], None, ALU.add)
                elif f in CONV:
                    m = CONV.index(f)
                    ins = low(cT_l[:, m, :], src[:, 0:SEQ], cT_h[:, m, :], bias[:, B_CONV + m:B_CONV + m + 1])
                elif f in HEADS_IN:
                    keys, m0 = HEADS_IN[f]
                    for t in range(2):
                        m, cols = m0 + t, slice(t * SEQ, (t + 1) * SEQ)
                        if not keys:
                            ins = low(qT_l[:, m, :], src[:, cols], qT_h[:, m, :], bias[:, B_Q + m:B_Q + m + 1])
                        else:
                            for rows in head_rows:
                                ins = low(key_place(kT_l, m, rows), src[rows, cols].rearrange("p (b n) -> p b n", b=ST),
                                          key_place(kT_h, m, rows), bias[rows, B_K + m:B_K + m + 1])
                else:
                    ins = low(vt_l[:, :, :].rearrange("p b n -> p (b n)"), src[:, 0:SEQ],
                              vt_h[:, :, :].rearrange("p b n -> p (b n)"))
                ins.then_inc(front_lo, 1)

            def maxima(s, u):
                for e in range(2):
                    dve.wait_ge(score_done, s * 2 * UNITS + (2 * u + e + 1))
                    ins = dve.tensor_reduce(row_max[:, u % 2, 4 * e:4 * e + 4],
                                            score_bank(s, u, e)[:, :].rearrange("p (k n) -> p k n", k=4), AX_X, ALU.max)
                ins.then_inc(max_found, 1)
                dve.wait_ge(max_found, s * UNITS + (u + 1))
                dve.tensor_scalar(neg_max[:, u % 2, :], row_max[:, u % 2, :], -SCALE, None,
                                  ALU.mult).then_inc(max_ready, 1)

            def probabilities(s, u):
                dve.wait_ge(exp_done, s * 2 * UNITS + (2 * u + 2))
                dve.reciprocal(inv_sum[:, u % 2, :], row_sum[:, u % 2, :]).then_inc(sum_inverted, 1)
                dve.wait_ge(sum_inverted, s * UNITS + (u + 1))
                p = probs[:, u % 2, :].rearrange("p (h n) -> p h n", h=GH)
                dve.tensor_tensor(p, p, inv_sum[:, u % 2, :].unsqueeze(2).broadcast_to([P, GH, BLK]),
                                  ALU.mult).then_inc(norm_done, 1)

            def probs_low(s, u):
                for e in range(2):
                    dve.wait_ge(turn_hi, s * 2 * UNITS + (2 * u + e + 1))
                    low(pT_l[:, e, :], ps_turn[e][:, :], pT_h[:, e, :]).then_inc(turn_lo, 1)

            def z_low(s, u):
                for e in range(2):
                    dve.wait_ge(z_hi, s * 2 * UNITS + (2 * u + e + 1))
                    low(zT_l[:, e, :, u % ST, :], ps_turn[e][:, :].rearrange("p (k n) -> p k n", k=4),
                        zT_h[:, e, :, u % ST, :]).then_inc(z_lo, 1)

            def y_low(s):
                dve.wait_ge(y_hi, s + 1)
                low(yT_l[:, :], ps_y[:, 0:SEQ], yT_h[:, :], out_bias[:, :]).then_inc(y_lo, 1)

            def output(s):
                dve.wait_ge(x_biased, s * ST + ST)
                for b in range(ST):
                    dve.wait_ge(out_done, s * ST + (b + 1))
                    tile = x[:, bass.ds(s * ST + b, 1), :].rearrange("p a n -> p (a n)")
                    dve.tensor_tensor(tile, ps_turn[b][:, :], tile, ALU.add).then_inc(x_attended, 1)

            def attend(s, n, after):
                def fronts(first, last):
                    for f in range(first, last):
                        front(n, f)

                norm_ahead = after is None
                if norm_ahead:
                    dve.wait_ge(x_attended, HT)
                    norm_sums(0)
                probabilities(s, 0)
                fronts(2, 3)
                maxima(s, 1)
                probs_low(s, 0)
                if norm_ahead:
                    norm_stats(0)
                probabilities(s, 1)
                fronts(3, 5)
                z_low(s, 0)
                fronts(5, 6)
                maxima(s, 2)
                fronts(6, 7)
                probs_low(s, 1)
                probabilities(s, 2)
                maxima(s, 3)
                z_low(s, 1)
                fronts(7, 9)
                probabilities(s, 3)
                probs_low(s, 2)
                fronts(9, 10)
                z_low(s, 2)
                fronts(10, 11)
                probs_low(s, 3)
                fronts(11, 12)
                z_low(s, 3)
                fronts(12, 13)
                if after is not None:
                    sequence_norm(after)
                if norm_ahead:
                    normalise(2)
                fronts(F_V, FRONT)
                y_low(s)
                maxima(n, 0)
                if after is not None:
                    for f in range(TURNED):
                        front(after, f)
                output(s)

            def attend_last(s):
                maxima(s, 1)
                probabilities(s, 0)
                maxima(s, 2)
                probs_low(s, 0)
                probabilities(s, 1)
                z_low(s, 0)
                maxima(s, 3)
                probs_low(s, 1)
                probabilities(s, 2)
                z_low(s, 1)
                probs_low(s, 2)
                probabilities(s, 3)
                z_low(s, 2)
                probs_low(s, 3)
                z_low(s, 3)
                xT_low(2, 0, KT - 1)
                y_low(s)
                w13_low(0, 2 * NT, 0)
                xT_low(2, KT - 1)
                output(s)

            def first_front():
                dve.wait_ge(w_saved, 16 * NT)
                for part in (xp_h, xp_l):
                    for column in (0, SEQ + 1):
                        dve.memset(part[:, :, column:column + 1].bitcast(F32), 0.0)
                for f in range(TURNED):
                    front(0, f)
                for q in range(4):
                    dve.wait_ge(m_hi, q + 1)
                    low(m_place(m_l, q), ps_m[q][:, :].rearrange("p (k n) -> p k n", k=4),
                        m_place(m_h, q)).then_inc(m_lo, 1)

            def step(i, base, b, split=True):
                if base == NT:
                    attw_low(i - 1, 1 - b)
                if split:
                    w13_low(i, base, b)
                hidden(i - 1, base, 1 - b)
                w2_low(i, base, b)

            def passes(p, carry_on):
                base = NT * p
                if p == 1:
                    dve.wait_ge(x_updated, HT)
                    norm_sums(0)
                step(1, base, 1, False)
                if p == 2:
                    norm_sums(1)
                with dve.Fori(1, NT // 2) as j:
                    step(j * 2, base, 0)
                    step(j * 2 + 1, base, 1)
                if p == 1:
                    norm_stats(0)
                    sequence_norm(0)
                if p == 2:
                    norm_stats(1)
                    normalise(3)
                if carry_on:
                    w13_low(0, base + NT, 0)
                hidden(NT - 1, base, 1)
                if carry_on:
                    next_half(p + 1)
                if p == 1:
                    first_front()
                update_x(p)

            def next_half(p):
                w2_low(0, NT * p, 0)
                xT_low(p)
                w13_low(1, NT * p, 1)

            def update_x(p):
                for t in range(HT):
                    if t == HT - 1:
                        dve.wait_ge(down_done, NT * (p + 1))
                    else:
                        dve.wait_ge(down_tile, (HT - 1) * p + t + 1)
                    tile = x[:, HT * p % (2 * HT) + t, :]
                    dve.scalar_tensor_tensor(out=tile, in0=acc[t][:, :], scalar=0.5, in1=tile, op0=ALU.mult,
                                             op1=ALU.add).then_inc(x_updated, 1)

            def total(m, n):
                dve.tensor_reduce(abs_tot[:, m:m + 1], abs_sum[:, m, 0:n], AX_X, ALU.add).then_inc(tot_ready, 1)

            def mean(m):
                dve.wait_ge(tot_sum, m + 1)
                link(dve.tensor_scalar(coeff[:, m:m + 1], ps_total[:, m:m + 1], 1.0 / (INTER * DM), None, ALU.mult))

            dve.wait_ge(x_loaded[0], 16)
            norm_sums(0)
            norm_stats(0)
            normalise(0)
            for k in range(CH1):
                sum_abs1(k)
                if k == 2:
                    xT_low(0)
            dve.wait_ge(abs_done, CH1)
            total(0, CH1)
            mean(0)
            dve.wait_ge(sign_done, CH1)

            def gate_step(t, tt, j):
                if tt + 1 < NT:
                    form(0, t + 1, w1_formed)
                early_low(0, t, tt)
                small_sum(t, tt, j)
                if isinstance(t, int) and t == 3:
                    dve.wait_ge(x_loaded[1], 16)
                    norm_sums(1)

            form(0, 0, w1_formed)
            ring_steps(dve, gate_step)
            dve.wait_ge(abs_done, before(2))
            total(1, NT)
            mean(1)
            dve.wait_ge(sign_done, before(2))

            def up_step(t, tt, j):
                if tt + 1 < NT:
                    form(1, t + 1, w3_formed)
                early_low(1, t, tt)
                if tt == NT - 1:
                    dve.wait_ge(sign_done, before(3))
                    total(2, NT)
                if tt >= 2:
                    hidden_early(t - 2, tt - 2)
                if isinstance(t, int) and t == 3:
                    norm_stats(1)

            form(1, 0, w3_formed)
            ring_steps(dve, up_step)
            mean(2)
            hidden_early(NT - 2, NT - 2)

            def down_step(i, b):
                form(2, i, w2_formed)
                hidden_early_low(i, b)
                w2_low(i, 0, b)

            down_step(0, 0)
            hidden_early(NT - 1, NT - 1)
            down_step(1, 1)
            normalise(1, 0, HT // 2)
            with dve.Fori(1, NT // 2) as j:
                down_step(j * 2, 0)
                down_step(j * 2 + 1, 1)
            normalise(1, HT // 2, HT)
            w13_low(0, NT, 0)
            next_half(1)
            update_x(0)
            passes(1, False)

            dve.wait_ge(aw_hi, AW + 1)
            low(pw_l[:, :], aw_raw[:, AW % 2, :], pw_h[:, :]).then_inc(aw_lo, 1)
            dve.wait_ge(small_loaded, 32)
            dve.wait_ge(x_updated, 2 * HT)
            norm_sums(1)
            front(0, 2)
            sequence_norm(1)
            for f in range(CONV[0] + 1, CONV[1] + 1):
                front(0, f)
            dve.wait_ge(bias_sum, 1)
            dve.tensor_tensor(out_bias[:, :], ps_turn[0][:, 0:1], bias[:, B_O:B_O + 1], ALU.add).then_inc(bias_ready, 1)
            norm_stats(1)
            for f in range(CONV[1] + 1, FRONT):
                front(0, f)
            for f in range(TURNED):
                front(1, f)
            maxima(0, 0)
            with dve.Fori(0, SEQS - 2) as s:
                attend(s, s + 1, s + 2)
            attend(SEQS - 2, SEQS - 1, None)
            attend_last(SEQS - 1)

            w2_low(0, 2 * NT, 0)
            w13_low(1, 2 * NT, 1)
            passes(2, True)
            passes(3, False)

        @block.tensor
        def _(pe):
            def product3(out, lhs, rhs, start, stop):
                pe.matmul(out, lhs[0], rhs[0], start=start, stop=False)
                pe.matmul(out, lhs[0], rhs[1], start=False, stop=False)
                return pe.matmul(out, lhs[1], rhs[0], start=False, stop=stop)

            def transpose_x(p):
                pe.wait_ge(xn_ready, p + 1)
                if p % 2:
                    pe.wait_ge(silu_done, NT * p)
                    pe.wait_ge(hid_ready, NT * p)
                turn_x(p, 0, KT)

            def turn_x(p, first, last_k):
                for k in range(first, last_k):
                    for t in range(HT):
                        last = pe.transpose(ps_xT[k][:, t * P:(t + 1) * P], xn[p][:, t, k * P:(k + 1) * P],
                                            ident[:, :])
                    last.then_inc(xT_done, 1)

            def width_product(out, b, m):
                for k in range(KT):
                    last = product3(out, [w[:, b, m, k * P:(k + 1) * P] for w in (w13_h, w13_l)],
                                    [v[:, k, :] for v in (xT_h, xT_l)], k == 0, k == KT - 1)
                return last

            def early_product(m, t, tt):
                n = m * NT + tt
                pe.wait_ge(w13_lo, t + (m * NT + 1))
                if m and tt >= 4:
                    pe.wait_ge(hid_ready, t - 3)
                else:
                    at_least(pe, silu_done, t + (m * NT - 3))
                if isinstance(t, int) and t == NT - 2:
                    sum_total(m + 1)
                out = bank[n % 4][:, :]
                for k in range(KT):
                    last = product3(out, [w[:, n % 2, n // 2 % 2, k * P:(k + 1) * P] for w in (w13_h, w13_l)],
                                    [v[:, k, :] for v in (xT_h, xT_l)], k == 0, k == KT - 1)
                last.then_inc(early_done, 1)

            def sum_total(m):
                pe.wait_ge(tot_ready, m + 1)
                pe.matmul(ps_total[:, m:m + 1], ones[:, :], abs_tot[:, m:m + 1],
                          start=True, stop=True).then_inc(tot_sum, 1)

            def gate_up(i, base, b):
                pe.wait_ge(w13_lo, i + (base + NT + 1))
                at_least(pe, silu_done, i + (base - 1))
                width_product(ps_gate[b][:, :], b, 0).then_inc(gate_done, 1)
                at_least(pe, hid_ready, i + (base - 1))
                width_product(ps_up[b][:, :], b, 1).then_inc(up_done, 1)

            def down(i, base, b, start, stop):
                pe.wait_ge(w2_lo, i + (base + 1))
                pe.wait_ge(hid_lo, i + (base + 1))
                if start:
                    at_least(pe, x_updated, HT * (base // NT))
                for t in range(HT):
                    ins = product3(acc[t][:, :], [h[:, b, t * P:(t + 1) * P] for h in (hid_h, hid_l)],
                                    [w[:, b, :] for w in (w2_h, w2_l)], start, stop)
                    if t == HT - 1:
                        ins.then_inc(down_done, 1)
                    elif stop:
                        ins.then_inc(down_tile, 1)

            def passes(p, carry_on):
                base = NT * p
                pe.wait_ge(xT_lo, KT * (p + 1))
                gate_up(0, base, 0)
                gate_up(1, base, 1)
                down(0, base, 0, True, False)
                with pe.Fori(1, NT // 2) as j:
                    gate_up(j * 2, base, 0)
                    down(j * 2 - 1, base, 1, False, False)
                    gate_up(j * 2 + 1, base, 1)
                    down(j * 2, base, 0, False, False)
                if carry_on:
                    transpose_x(p + 1)
                if p == 1:
                    first_front()
                down(NT - 1, base, 1, False, True)

            def front_bank(n, f):
                previous = f - 3 if f >= 3 else -1 - (FRONT - 1 - f) % 3
                at_least(pe, front_lo, n * FRONT + (previous + 1))
                return ps_front[f % 3]

            def turn_tokens(n):
                pe.wait_ge(xs_ready, n + 1)
                for f in range(TURNED):
                    dst = front_bank(n, f)
                    for k in range(2):
                        for b in range(ST):
                            last = pe.transpose(dst[:, (k * ST + b) * P:(k * ST + b + 1) * P],
                                                xs[:, b, (2 * f + k) * P:(2 * f + k + 1) * P], ident[:, :])
                    last.then_inc(front_done, 1)

            def conv(n, m, first=0, last=KT):
                f = CONV[m]
                dst = front_bank(n, f) if first == 0 else ps_front[f % 3]
                for k in range(first, last):
                    if m == 0:
                        pe.wait_ge(front_lo, n * FRONT + (k // 2 + 1))
                    for tap in range(TAPS):
                        ins = product3(dst[:, 0:SEQ], [conv_w(w, tap, k, m) for w in (aw_h, aw_l)],
                                       [v[:, k, tap:tap + SEQ] for v in (xp_h, xp_l)],
                                       k == 0 and tap == 0, k == KT - 1 and tap == TAPS - 1)
                if last == KT:
                    ins.then_inc(front_done, 1)

            def heads_of(n, f):
                c, m0 = HEADS_IN[f]
                col = (Q_COL, K_COL)[c]
                pe.wait_ge(front_lo, n * FRONT + (CONV[c] + 1))
                dst = front_bank(n, f)
                for e in range(2):
                    m = m0 + e
                    last = product3(dst[:, e * SEQ:(e + 1) * SEQ], [columns(w, col + m * P, P) for w in (aw_h, aw_l)],
                                    [v[:, c, :] for v in (cT_h, cT_l)], True, True)
                last.then_inc(front_done, 1)

            def turn_values(n):
                pe.wait_ge(front_lo, n * FRONT + (F_CV + 1))
                dst = front_bank(n, F_V)
                for b in range(ST):
                    last = pe.transpose(dst[:, b * BLK:(b + 1) * BLK], cv[:, b * BLK:(b + 1) * BLK], ident[:, :])
                last.then_inc(front_done, 1)

            def scores(s, u, banks=(0, 1)):
                g, b = u // ST, u % ST
                last_sequence = isinstance(s, int) and s == SEQS - 1
                for i in banks:
                    dst = score_bank(s, u, i)
                    pe.wait_ge(front_lo, s * FRONT + (KEYS_OF[4 * g + 2 * i] + 1))
                    previous = u - 2 if last_sequence and u else u - 1
                    if not (last_sequence and u == 1):
                        at_least(pe, exp_done, s * 2 * UNITS + (2 * previous + i + 1))
                    pe.matmul(dst[:, :], ident_r[:, :], mask_r[:, :, :].rearrange("p a n -> p (a n)"),
                              start=True, stop=False)
                    for t in range(2):
                        last = product3(dst[:, 2 * t * BLK:2 * (t + 1) * BLK],
                                        [v[:, 4 * g + 2 * i + t, b * BLK:(b + 1) * BLK] for v in (qT_h, qT_l)],
                                        [v[g][:, 2 * i + t, b, :, :].rearrange("p e n -> p (e n)")
                                         for v in (kT_h, kT_l)],
                                        False, t == 1)
                    last.then_inc(score_done, 1)

            def turn_probs(s, u):
                pe.wait_ge(norm_done, s * UNITS + (u + 1))
                for e in range(2):
                    if u:
                        pe.wait_ge(z_lo, s * 2 * UNITS + (2 * u + e - 1))
                    for k in range(4):
                        last = pe.transpose(ps_turn[e][:, k * BLK:(k + 1) * BLK],
                                            probs[:, u % 2, (4 * e + k) * BLK:(4 * e + k + 1) * BLK], ident[:, :])
                    last.then_inc(turn_done, 1)

            def attended(s, u):
                if u == 0:
                    pe.wait_ge(front_lo, s * FRONT + FRONT)
                for e in range(2):
                    pe.wait_ge(turn_lo, s * 2 * UNITS + (2 * u + e + 1))
                    product3(ps_turn[e][:, :], [v[:, u % ST, :] for v in (vt_h, vt_l)],
                             [v[:, e, :] for v in (pT_h, pT_l)], True, True).then_inc(z_done, 1)

            def group_output(s, g):
                for e in range(2):
                    pe.wait_ge(z_lo, s * 2 * UNITS + (4 * g + 3 + e))
                    for k in range(4):
                        h = GH * g + 4 * e + k
                        last = product3(ps_y[:, 0:SEQ], [v[:, h, :] for v in (m_h, m_l)],
                                        [v[:, e, k, :, :].rearrange("p b n -> p (b n)") for v in (zT_h, zT_l)],
                                        h == 0, h == HEADS - 1)
                if g:
                    last.then_inc(y_done, 1)

            def project(s):
                pe.wait_ge(y_lo, s + 1)
                for b in range(ST):
                    product3(ps_turn[b][:, :], [v[:, b * BLK:(b + 1) * BLK] for v in (yT_h, yT_l)],
                             [v[:, :] for v in (pw_h, pw_l)], True, True).then_inc(out_done, 1)

            def attend(s, n, after):
                def heads(*fills):
                    for f in fills:
                        heads_of(n, f)

                conv(n, 0)
                scores(s, 1)
                turn_probs(s, 0)
                heads(3, 4)
                conv(n, 1, 0, KT // 2)
                attended(s, 0)
                conv(n, 1, KT // 2, KT)
                scores(s, 2)
                heads(6)
                turn_probs(s, 1)
                heads(7)
                conv(n, 2, 0, KT // 2)
                attended(s, 1)
                scores(s, 3)
                conv(n, 2, KT // 2, KT)
                turn_probs(s, 2)
                heads(9)
                group_output(s, 0)
                attended(s, 2)
                heads(10)
                turn_probs(s, 3)
                heads(11, 12)
                scores(n, 0, (0,))
                attended(s, 3)
                scores(n, 0, (1,))
                turn_values(n)
                group_output(s, 1)
                if after is not None:
                    turn_tokens(after)
                project(s)

            def attend_last(s):
                pe.wait_ge(front_lo, SEQS * FRONT)
                scores(s, 1)
                scores(s, 2)
                turn_probs(s, 0)
                scores(s, 3)
                attended(s, 0)
                turn_probs(s, 1)
                attended(s, 1)
                turn_probs(s, 2)
                group_output(s, 0)
                attended(s, 2)
                turn_probs(s, 3)
                pe.wait_ge(xn_ready, 3)
                pe.wait_ge(exp_done, SEQS * 2 * UNITS)
                turn_x(2, 0, KT - 1)
                attended(s, 3)
                group_output(s, 1)
                pe.wait_ge(y_lo, s + 1)
                turn_x(2, KT - 1, KT)
                project(s)

            def first_front():
                pe.wait_ge(silu_done, 2 * NT)
                turn_tokens(0)
                pe.wait_ge(hid_ready, 2 * NT)
                for q in range(4):
                    g, rows = q // 2, head_rows[q % 2]
                    pe.wait_ge(mraw_loaded[g], 16)
                    at_least(pe, m_lo, q - 1)
                    for k in range(4):
                        cols = slice(k * W, (k + 1) * W)
                        last = pe.matmul(ps_m[q][:, cols], mraw[g][rows, 0, cols], mraw[g][rows, 1, cols],
                                         start=True, stop=True)
                    last.then_inc(m_done, 1)

            pe.wait_ge(const_ready, 3)
            transpose_x(0)
            sum_total(0)
            pe.wait_ge(xT_lo, KT)
            for m in range(2):
                ring_steps(pe, lambda t, tt, j: early_product(m, t, tt))
            down(0, 0, 0, True, False)
            with pe.Fori(1, NT // 2) as j:
                down(j * 2 - 1, 0, 1, False, False)
                down(j * 2, 0, 0, False, False)
            transpose_x(1)
            down(NT - 1, 0, 1, False, True)
            passes(1, False)

            pe.wait_ge(m_lo, 4)
            conv(0, 0)
            heads_of(0, 3)
            heads_of(0, 4)
            conv(0, 1)
            pe.wait_ge(small_loaded, 32)
            pe.wait_ge(x_updated, 2 * HT)
            for m in range(MT):
                last = pe.matmul(ps_turn[0][:, 0:1], mraw[m // 4][:, 1, m % 4 * P:(m % 4 + 1) * P],
                                 bias[:, B_V + m:B_V + m + 1], start=m == 0, stop=m == MT - 1)
            last.then_inc(bias_sum, 1)
            heads_of(0, 6)
            heads_of(0, 7)
            conv(0, 2)
            for f in range(9, 13):
                heads_of(0, f)
            pe.wait_ge(consts_r, 2)
            pe.wait_ge(aw_lo, AW + 1)
            pe.wait_ge(bias_ready, 1)
            pe.wait_ge(zeros_ready, 8)
            scores(0, 0, (0,))
            turn_values(0)
            turn_tokens(1)
            scores(0, 0, (1,))
            with pe.Fori(0, SEQS - 2) as s:
                attend(s, s + 1, s + 2)
            attend(SEQS - 2, SEQS - 1, None)
            attend_last(SEQS - 1)
            passes(2, True)
            passes(3, False)


def kernel(**inputs):
    import numpy as _np
    import concourse.bacc as _bacc
    from concourse.bass_utils import run_bass_kernel_spmd as _run

    a = {n[3:]: _np.asarray(v) for n, v in inputs.items()}

    def inner_cols(w):
        return w.reshape(NT, P, KT, P).transpose(3, 0, 2, 1).reshape(P, NT, DM)

    def inner_rows(w):
        return w.reshape(DM, NT, P).transpose(2, 1, 0)

    def columns(v):
        return v.reshape(-1, P).T

    wv = a["attn_wv"].transpose(1, 2, 0).reshape(2, MT // 2, P, W)
    wo = a["attn_wo"].reshape(2, MT // 2, P, W)
    attw = [a["attn_conv_w"].reshape(TAPS * KT, P, CONV_OUT).transpose(1, 0, 2), a["attn_wk"], a["attn_wq"],
            a["attn_proj_w"], _np.stack([wv, wo], axis=1).transpose(3, 0, 1, 2, 4)]
    biases = [columns(a["attn_" + n]) for n in ("conv_b", "bq", "bk", "bv", "bo")]
    arrays = {
        "x": a["attn_inputs"].reshape(TOK, DM),
        "w": _np.concatenate([inner_cols(a["ffn_w1"]), inner_cols(a["ffn_w3"]), inner_rows(a["ffn_w2"])],
                             axis=1).reshape(P, 3 * NT * DM),
        "base": _np.concatenate([inner_cols(a["ffn_mean_w1"]), inner_cols(a["ffn_mean_w3"]),
                                 inner_rows(a["ffn_mean_w2"])], axis=1).reshape(P, 3 * NT * DM),
        "attw": _np.concatenate([v.reshape(P, -1) for v in attw], axis=1),
        "bias": _np.concatenate(biases, axis=1),
        "projb": a["attn_proj_b"],
    }
    arrays = {n: _np.ascontiguousarray(v) for n, v in arrays.items()}
    nc = _bacc.Bacc("TRN2", target_bir_lowering=False, num_devices=1, dynamic_dma_scratch_size=512)
    args = [nc.dram_tensor(n, v.shape, F32, kind="ExternalInput").ap() for n, v in arrays.items()]
    scratch = nc.dram_tensor("formed_weights", (P, NT * 3 * DM), F32, kind="Internal").ap()
    out = nc.dram_tensor("out", (TOK, DM), F32, kind="ExternalOutput").ap()
    macaron(nc, *args, scratch, out)
    r = _run(nc, [arrays], core_ids=[0])
    return r.results[0]["out"].reshape(SEQS, SEQ, DM)
```
